# Optimizing a Trainium2 kernel written in Bass

```python
import numpy as np
import jax
import jax.numpy as jnp

def _softmax(x, axis=-1):
    return jax.nn.softmax(x, axis=axis)

def _gelu(x):
    return jax.nn.gelu(x, approximate=True)

def _silu(x):
    return jax.nn.silu(x)

def _sigmoid(x):
    return jax.nn.sigmoid(x)

def _layernorm(x, axis=-1, eps=1e-05):
    m = jnp.mean(x, axis=axis, keepdims=True)
    v = jnp.var(x, axis=axis, keepdims=True)
    return (x - m) / jnp.sqrt(v + eps)

def _scatter_add(tgt, idx, src, axis=0):
    return tgt.at[idx].add(src)

def _segment_sum(src, seg, n):
    return jax.ops.segment_sum(src, seg, n)
kernel_name = 'mk_cond_resid_d2_seqx_r2_c152d2'

def setup_inputs(seed: int=0):
    np.random.seed(seed)
    _w = jnp.asarray

    def _rec_inputs():
        import jax
        import jax.numpy as jnp
        _rk = jax.random.key(seed)
        x = 8.748e-05 + 1 * jax.random.normal(jax.random.fold_in(_rk, 1), (4, 1024, 1024), jnp.float32)
        _lenS = 1024 - jax.random.randint(jax.random.fold_in(_rk, 7), (4,), 0, max(1, 1024 // 4) + 1, jnp.int32)
        _lenS2 = 1024 - jax.random.randint(jax.random.fold_in(_rk, 8), (4,), 0, max(1, 1024 // 4) + 1, jnp.int32)
        fside_BxSx1_0 = -0.00499425 + 1.0058 * jax.random.normal(jax.random.fold_in(_rk, 11), (4, 1024, 1), jnp.float32)
        cond_2048 = 0.00513981 + 1.0024 * jax.random.normal(jax.random.fold_in(_rk, 12), (4, 1024), jnp.float32)
        return (x, fside_BxSx1_0, cond_2048)
    x, fside_BxSx1_0, cond_2048 = _rec_inputs()

    def _L0_cond_setup():
        import jax, jax.numpy as jnp
        import numpy as np
        G, N, K = (16, 1024, 10240)
        key = jax.random.key(seed)
        k1, k2, k3 = jax.random.split(key, 3)
        return {'emb_s': jax.random.normal(k1, (G, N, 1), dtype=jnp.float32), 'emb_t': jax.random.normal(k2, (G, 1, N), dtype=jnp.float32), 'attention_weights': jax.random.normal(k3, (G, N, N), dtype=jnp.float32), 'k': K}
    _L0_cond_all = _L0_cond_setup()
    _L0_cond_in = {k: v for k, v in _L0_cond_all.items() if k in ()}
    del _L0_cond_all

    def _L1_cond_setup():
        import jax, jax.numpy as jnp
        import numpy as np
        HEADS = 16
        EPS = 1e-06

        def _rms_norm(x, g):
            xf = x.astype(jnp.float32)
            y = xf * jax.lax.rsqrt(jnp.mean(xf * xf, axis=-1, keepdims=True) + EPS)
            return y.astype(x.dtype) * g
        key = jax.random.key(seed)
        ks = jax.random.split(key, 6)
        b, n, dim, emb_dim = (4, 1024, 1024, 1024)
        d_head = dim // HEADS
        return {'x': jax.random.normal(ks[0], (b, n, dim), jnp.float32), 'emb': jax.random.normal(ks[1], (b, 1, emb_dim), jnp.float32), 'W_emb': jax.random.normal(ks[2], (emb_dim, 2 * dim), jnp.float32) * emb_dim ** (-0.5), 'b_emb': jnp.zeros((2 * dim,), jnp.float32), 'g_norm': jnp.ones((dim,), jnp.float32), 'W_qkv': jax.random.normal(ks[3], (dim, 3 * dim), jnp.float32) * dim ** (-0.5), 'g_q': jnp.ones((d_head,), jnp.float32), 'g_k': jnp.ones((d_head,), jnp.float32), 'W_out': jax.random.normal(ks[4], (dim, dim), jnp.float32) * dim ** (-0.5)}
    _L1_cond_all = _L1_cond_setup()
    _L1_cond_in = {k: v for k, v in _L1_cond_all.items() if k in ('W_emb', 'b_emb', 'g_norm', 'W_qkv', 'g_q', 'g_k', 'W_out')}
    del _L1_cond_all
    return {'x': x, 'fside_BxSx1_0': fside_BxSx1_0, 'cond_2048': cond_2048, 'L1_cond_W_emb': _L1_cond_in['W_emb'], 'L1_cond_b_emb': _L1_cond_in['b_emb'], 'L1_cond_g_norm': _L1_cond_in['g_norm'], 'L1_cond_W_qkv': _L1_cond_in['W_qkv'], 'L1_cond_g_q': _L1_cond_in['g_q'], 'L1_cond_g_k': _L1_cond_in['g_k'], 'L1_cond_W_out': _L1_cond_in['W_out']}

def reference(x, fside_BxSx1_0, cond_2048, L1_cond_W_emb, L1_cond_b_emb, L1_cond_g_norm, L1_cond_W_qkv, L1_cond_g_q, L1_cond_g_k, L1_cond_W_out):
    import jax
    import jax.numpy as jnp

    def _L0_cond_ref(emb_s, emb_t, attention_weights, k):
        import jax, jax.numpy as jnp
        import numpy as np
        G, N, K = (16, 1024, 10240)
        g, n = (emb_s.shape[0], emb_s.shape[1])
        adj = emb_s * emb_t
        att = jax.nn.softmax(attention_weights, axis=-1) * (1.0 / np.sqrt(n).astype(np.float32))
        adj = adj * att
        diag = jnp.arange(n)
        adj = adj.at[:, diag, diag].set(-jnp.inf)
        flat = adj.reshape(g, n * n)
        _, idx = jax.lax.top_k(flat, k)
        rows = jnp.arange(g)[:, None]
        out = jnp.zeros((g, n * n), dtype=adj.dtype).at[rows, idx].set(1.0)
        return out.reshape(g, n, n)

    def _L1_cond_ref(x, emb, W_emb, b_emb, g_norm, W_qkv, g_q, g_k, W_out):
        import jax, jax.numpy as jnp
        import numpy as np
        HEADS = 16
        EPS = 1e-06

        def _rms_norm(x, g):
            xf = x.astype(jnp.float32)
            y = xf * jax.lax.rsqrt(jnp.mean(xf * xf, axis=-1, keepdims=True) + EPS)
            return y.astype(x.dtype) * g
        b, n, dim = x.shape
        h = HEADS
        d = dim // h
        scale_shift = emb @ W_emb + b_emb
        scale, shift = jnp.split(scale_shift, 2, axis=-1)
        xn = _rms_norm(x, g_norm) * (1.0 + scale) + shift
        qkv = xn @ W_qkv
        qkv = qkv.reshape(b, n, 3, h, d)
        q, k, v = jnp.moveaxis(qkv, 2, 0)
        q = jnp.swapaxes(q, 1, 2)
        k = jnp.swapaxes(k, 1, 2)
        v = jnp.swapaxes(v, 1, 2)
        q = _rms_norm(q, g_q)
        k = _rms_norm(k, g_k)
        logits = jnp.einsum('bhqd,bhkd->bhqk', q, k) * d ** (-0.5)
        attn = jax.nn.softmax(logits, axis=-1)
        o = jnp.einsum('bhqk,bhkd->bhqd', attn, v)
        o = jnp.swapaxes(o, 1, 2).reshape(b, n, dim)
        return o + o @ W_out
    x = x + _L0_cond_ref(fside_BxSx1_0, cond_2048[:, None, :], x, 10240)
    x = x + _L1_cond_ref(x, cond_2048[:, None, :], L1_cond_W_emb, L1_cond_b_emb, L1_cond_g_norm, L1_cond_W_qkv, L1_cond_g_q, L1_cond_g_k, L1_cond_W_out)
    return x

_drawn_inputs = setup_inputs


def setup_inputs(seed=0):
    import zlib

    import numpy as np

    out = dict(_drawn_inputs(seed))
    spreads = {'L1_cond_b_emb': (0.0, 0.1),
     'L1_cond_g_norm': (1.0, 0.6),
     'L1_cond_g_q': (1.0, 0.6),
     'L1_cond_g_k': (1.0, 0.6)}
    factors = {}
    for name, (base, spread) in spreads.items():
        noise = np.random.default_rng([zlib.crc32(name.encode()), seed]).standard_normal(out[name].shape)
        drawn = base * np.exp(spread * noise) if base else spread * noise
        out[name] = jnp.asarray(drawn.astype(out[name].dtype))
    for name, factor in factors.items():
        out[name] = (out[name] * factor).astype(out[name].dtype)
    return out
```

```python
from contextlib import ExitStack

import concourse.bass as bass
from concourse import mybir

F32 = mybir.dt.float32
F32R = mybir.dt.float32r
I32 = mybir.dt.int32
U8 = mybir.dt.uint8
ALU = mybir.AluOpType
ACT = mybir.ActivationFunctionType
AX = mybir.AxisListType.X
ADD_ALL = bass.bass_isa.ReduceOp.add
P = 128
LOWEST = -3.4028234663852886e38
SIGN = -2147483648


def wait(e, sem, value):
    if not isinstance(value, int) or value > 0:
        e.wait_ge(sem, value)


def wait_apart(e, sem, value, passed):
    e.wait_ge(sem, value)
    e.sem_inc(passed, 1)


def cond_block(nc, x, s_in, cond, w_emb, b_emb, g_norm, w_qkv, g_q, g_k, w_out, out, ctx):
    B, N, D = x.shape
    T = N // P
    KT = D // P
    DH = g_q.shape[0]
    HEADS = D // DH
    PAIRS = HEADS // 2
    TOPK = 10240
    STEPS = 32
    EPS = 1e-6
    HALF = N // 2
    CHUNK = T * N // 4
    NC = B * KT
    assert T == 8 and KT == 8 and PAIRS == 8 and HALF == 512 and DH == 64

    def sem(name):
        return ctx.enter_context(nc.semaphore(name))

    def sb(name, shape, dt=F32):
        return ctx.enter_context(nc.sbuf_tensor(name, shape, dt))

    keys = sb("keys", [P, T, N])
    feat = sb("feat", [P, 2 * KT, N])
    xnT, oT = feat[:, 0:KT, :], feat[:, KT:2 * KT, :]
    wemb_v = feat[:].rearrange("p k n -> p (k n)").rearrange("p (k n) -> p k n", k=KT)
    wq = sb("wq", [P, KT, 3, P])
    v2 = sb("v2", [P, 2, T, 2, DH + 1])
    pt = sb("pt", [P, 2, N])
    stage = sb("stage", [P, 2, 4, P], F32R)
    sq = sb("sq", [P, 4, DH])
    qkn = sb("qkn", [P, 4, DH])
    otok = sb("otok", [P, T, P])
    trash = sb("trash", [P, 2, CHUNK], U8)
    gqk = sb("gqk", [P, 2, DH])
    ident = sb("ident", [P, P])
    identr = sb("identr", [P, P], F32R)
    tri = sb("tri", [P, P])
    mz = sb("mz", [P, 2, DH + T], F32R)
    params = sb("params", [NC + 24, P])
    paramsT = sb("paramsT", [P, NC + 24])
    gain = sb("gain", [P, 2 * KT, B])
    s_sb = sb("s_sb", [P, B, T])
    small = {n: sb(n, [P, w]) for n, w in dict(
        ss=4, rs=4, half4=4, rl=T, kmx=T, knm=T, kz=T, krz=T, kw=T, cnt=8, tot4=4, tot=1, gt4=4, ngt=1,
        pre=1, r0=1, rank=1, carry=1, ssx=T, rsx=T).items()}
    ss, rs, half4, rl = (small[n] for n in ("ss", "rs", "half4", "rl"))
    kmx, knm, kz, krz, kw = (small[n] for n in ("kmx", "knm", "kz", "krz", "kw"))
    cnt, tot4, tot, gt4, ngt, pre, r0, rank, carry, ssx, rsx = (
        small[n] for n in ("cnt", "tot4", "tot", "gt4", "ngt", "pre", "r0", "rank", "carry", "ssx", "rsx"))
    prefix, bit, cand, flip, thr, acc = (sb(n, [P, 1], I32) for n in ("prefix", "bit", "cand", "flip", "thr", "acc"))
    thr_f = thr[:].bitcast(F32)
    inner = ExitStack()
    sB0 = inner.enter_context(nc.sbuf_tensor("sB0", [P, 4, N], F32R))
    sA0 = inner.enter_context(nc.sbuf_tensor("sA0", [P, 4, N], F32R))
    sB1 = inner.enter_context(nc.sbuf_tensor("sB1", [P, 4, N], F32R))
    sA1 = inner.enter_context(nc.sbuf_tensor("sA1", [P, 4, N], F32R))
    inner.close()
    sA, sB = [sA0, sA1], [sB0, sB1]
    wo = sb("wo", [P, KT, N])
    xin = sb("xin", [P, 2, N])
    xr = sb("xr", [P, 4, N])
    eqm = sb("eqm", [P, N])
    scn = sb("scn", [P, N])
    tb = eqm
    xres, yout = pt[:, 0, :], pt[:, 1, :]

    pst = ctx.enter_context(nc.psum_tensor("pst", [P, 4, HALF], F32))
    ppv = ctx.enter_context(nc.psum_tensor("ppv", [P, 2, HALF], F32))
    pax = ctx.enter_context(nc.psum_tensor("pax", [P, 2, HALF], F32))
    paxr = pax[:].bitcast(F32R)

    d_par, d_wemb, d_gqk, d_s, d_tb, d_w, d_wo = (sem(n) for n in ("d_par", "d_wemb", "d_gqk", "d_s", "d_tb", "d_w", "d_wo"))
    d_key = [sem(f"d_key{t}") for t in range(T)]
    d_xin = [sem(f"d_xin{t}") for t in range(2)]
    d_x1 = [sem(f"d_x1{t}") for t in range(2)]
    d_res = [sem(f"d_res{t}") for t in range(2)]
    d_y = [sem(f"d_y{t}") for t in range(2)]
    c_pool, c_cst, c_par, c_parT, c_cnd, c_cndT = (sem(n) for n in ("c_pool", "c_cst", "c_par", "c_parT", "c_cnd", "c_cndT"))
    k_max, k_key, k_exp, k_diag = sem("k_max"), sem("k_key"), sem("k_exp"), sem("k_diag")
    passed = sem("passed")
    z_init, z_cnt, z_sum, z_up = sem("z_init"), sem("z_cnt"), sem("z_sum"), sem("z_up")
    f_dve, f_sum, f_tri, f_x1, f_sq, f_rs, f_xr, f_xt, f_ev = (
        sem(n) for n in ("f_dve", "f_sum", "f_tri", "f_x1", "f_sq", "f_rs", "f_xr", "f_xt", "f_ev"))
    a_qkv, a_sq, a_v, a_ss, a_rs, a_nm, a_tr, a_evB, a_evA, a_row = (
        sem(n) for n in ("a_qkv", "a_sq", "a_v", "a_ss", "a_rs", "a_nm", "a_tr", "a_evB", "a_evA", "a_row"))
    m_s, m_mx, m_row, m_ev = sem("m_s"), sem("m_mx"), sem("m_row"), sem("m_ev")
    t_st, t_ex, t_pv, t_rl, t_on, t_ot, t_oe = (sem(n) for n in ("t_st", "t_ex", "t_pv", "t_rl", "t_on", "t_ot", "t_oe"))
    o_wi, o_mm, o_add = sem("o_wi"), sem("o_mm"), sem("o_add")

    x_v = x.rearrange("b (p t) n -> b p t n", t=T)
    out_v = out.rearrange("b (p t) n -> b p t n", t=T)
    wqkv_v = w_qkv.rearrange("(k p) (s i c) -> p k s i c", p=P, s=3, i=PAIRS)

    CST = 2

    class Sync:
        def __init__(self, e):
            self.e = e

        def setup(self):
            e = self.e
            self.load_keys(0)
            e.dma_start(params[0:NC, :], cond.rearrange("b (k p) -> (b k) p", p=P)).then_inc(d_par, 16)
            e.dma_start(params[NC:NC + 16, :], b_emb.rearrange("(k p) -> k p", p=P)).then_inc(d_par, 16)
            e.dma_start(params[NC + 16:NC + 24, :], g_norm.rearrange("(k p) -> k p", p=P)).then_inc(d_par, 16)
            e.dma_start(s_sb[:], s_in.rearrange("b (p t) a -> p b (t a)", t=T)).then_inc(d_s, 16)
            e.dma_start(gqk[:, 0, :], g_q.partition_broadcast(P)).then_inc(d_gqk, 16)
            e.dma_start(gqk[:, 1, :], g_k.partition_broadcast(P)).then_inc(d_gqk, 16)
            e.dma_start(wemb_v, w_emb.rearrange("(k p) n -> p k n", p=P)).then_inc(d_wemb, 16)
            self.load_w(0)

        def load_keys(self, b):
            e = self.e
            for t in range(T):
                e.dma_start(keys[:, t, :], x_v[b, :, t, :]).then_inc(d_key[t], 16)
            e.dma_start(tb[:], cond[b, :].partition_broadcast(P)).then_inc(d_tb, 16)

        def load_w(self, i):
            for s in range(3):
                self.e.dma_start(wq[:, :, s, :], wqkv_v[:, :, s, i, :]).then_inc(d_w, 16)

        def search_alone(self, b):
            pass

        def x_tile(self, b, t):
            self.e.dma_start(xin[:, t % 2, :], x_v[b, :, t, :]).then_inc(d_xin[t % 2], 16)

        def finalise_tile(self, b, t):
            e = self.e
            e.wait_ge(f_x1, T * b + t + 1)
            e.dma_start(out_v[b, :, t, :], xin[:, t % 2, :]).then_inc(d_x1[t % 2], 16)
            if t + 2 < T:
                e.wait_ge(d_x1[t % 2], 16 * (T // 2 * b + t // 2 + 1))
                e.wait_ge(f_xr, T * b + t + 1)
                self.x_tile(b, t + 2)

        def boundary(self, ob, fb):
            e = self.e
            if ob is not None:
                wait_apart(e, t_pv, CST + T * 2 * PAIRS * (ob + 1), passed)
                for j in range(2):
                    e.wait_ge(d_x1[j], 16 * (T // 2) * (ob + 1))
                for c in range(2):
                    self.residual(ob, 0, c)
            if fb is not None:
                self.x_tile(fb, 0)
                self.x_tile(fb, 1)
            for t in range(T):
                if fb is not None:
                    self.finalise_tile(fb, t)
                if ob is not None:
                    for c in range(2):
                        e.wait_ge(o_add, 2 * T * ob + 2 * t + c + 1)
                        e.dma_start(out_v[ob, :, t, c * HALF:(c + 1) * HALF],
                                    yout[:, c * HALF:(c + 1) * HALF]).then_inc(d_y[c], 16)
                        if t + 1 < T:
                            self.residual(ob, t + 1, c)

        def residual(self, b, t, c):
            self.e.dma_start(xres[:, c * HALF:(c + 1) * HALF],
                             out_v[b, :, t, c * HALF:(c + 1) * HALF]).then_inc(d_res[c], 16)

        def prep_alone(self, b, kb):
            e = self.e
            if kb is not None:
                e.wait_ge(f_xr, T * (b + 1))
                self.load_keys(kb)
            e.wait_ge(a_qkv, T * (PAIRS * b + 1))
            self.load_w(1)

        def pair(self, b, i, par, search, prep, first):
            e, gp = self.e, PAIRS * b + i
            if prep:
                wait_apart(e, a_qkv, T * (gp + 2), passed)
                self.load_w((i + 2) % PAIRS)
            else:
                e.wait_ge(t_pv, CST + 2 * T * gp)
                e.dma_start(wo[:], w_out.rearrange("(k p) n -> p k n", p=P)).then_inc(d_wo, 16)

        def finish(self):
            for c in range(2):
                self.e.wait_ge(d_y[c], 16 * T * B)
                self.e.wait_ge(d_x1[c], 16 * T // 2 * B)

    class Pool:
        def __init__(self, e):
            self.e = e

        def setup(self):
            e = self.e
            e.memset(ident[:], 0.0).then_inc(c_pool, 1)
            e.memset(tri[:], 1.0).then_inc(c_pool, 1)
            e.memset(half4[:], -0.5).then_inc(c_pool, 1)
            e.wait_ge(c_pool, 3)
            e.affine_select(out=ident[:], in_=ident[:], compare_op=ALU.not_equal, fill=1.0, base=0,
                            pattern=[[-1, P]], channel_multiplier=1).then_inc(c_pool, 1)
            e.affine_select(out=tri[:], in_=tri[:], compare_op=ALU.is_gt, fill=0.0, base=0,
                            pattern=[[1, P]], channel_multiplier=-1).then_inc(c_pool, 1)
            e.memset(v2[:, :, :, :, DH:DH + 1], 1.0).then_inc(c_pool, 1)
            for t in range(T):
                self.keys_tile(0, t)

        def keys_tile(self, b, t):
            e, k = self.e, T * b + t
            wait_apart(e, k_key, 3 * k + 3, passed)
            e.affine_select(out=keys[:, t, :], in_=keys[:, t, :], compare_op=ALU.not_equal, fill=LOWEST,
                            base=t, pattern=[[-1, N]], channel_multiplier=T).then_inc(k_diag, 1)
            wait_apart(e, k_diag, k + 1, passed)

        def search_alone(self, b):
            with self.e.Fori(0, STEPS) as st:
                self.search_sum(STEPS * b + st)

        def search_sum(self, z):
            e = self.e
            wait_apart(e, z_cnt, CST + 4 * z + 4, passed)
            e.partition_all_reduce(tot4[:], cnt[:, 0:4], P, ADD_ALL).then_inc(z_sum, 1)

        def boundary(self, ob, fb):
            if fb is None:
                return
            e = self.e
            wait_apart(e, f_dve, F_STEPS * fb + 4, passed)
            e.partition_all_reduce(gt4[:], cnt[:, 0:4], P, ADD_ALL).then_inc(f_sum, 1)
            for t in range(T):
                n = T * fb + t
                wait_apart(e, f_sq, n + 1, passed)
                e.tensor_scalar(rsx[:, t:t + 1], ssx[:, t:t + 1], 1.0 / D, EPS, ALU.mult, ALU.add).then_inc(f_rs, 1)
                e.wait_ge(f_rs, 2 * n + 1)
                e.tensor_tensor(rsx[:, t:t + 1], rsx[:, t:t + 1], half4[:, 0:1], ALU.pow).then_inc(f_rs, 1)

        def prep_tile(self, gp, t):
            e, u = self.e, T * gp + t
            wait_apart(e, a_ss, u + 1, passed)
            e.tensor_scalar(rs[:], ss[:], 1.0 / DH, EPS, ALU.mult, ALU.add).then_inc(a_rs, 1)
            e.wait_ge(a_rs, 2 * u + 1)
            e.tensor_tensor(rs[:], rs[:], half4[:], ALU.pow).then_inc(a_rs, 1)

        def prep_rows(self, gp, par):
            e = self.e
            wait_apart(e, a_qkv, T * gp + 1, passed)
            e.memset(sA[par][DH:DH + 1, 0:2, :].bitcast(F32), 0.0).then_inc(a_row, 1)
            e.memset(sA[par][DH:DH + 1, 2:4, :].bitcast(F32), -1.0).then_inc(a_row, 1)
            wait_apart(e, a_row, 2 * (gp + 1), passed)

        def prep_alone(self, b, kb):
            gp = PAIRS * b
            self.prep_rows(gp, 0)
            for t in range(T):
                self.prep_tile(gp, t)
                if kb is not None and t > 0:
                    self.keys_tile(kb, t - 1)
            if kb is not None:
                self.keys_tile(kb, T - 1)

        def pair(self, b, i, par, search, prep, first):
            gp = PAIRS * b + i
            if prep:
                self.prep_rows(gp + 1, 1 - par)
            for t in range(T):
                if search and t % 2 == 1:
                    self.search_sum(STEPS * (b + 1) + 4 * i + t // 2)
                if prep:
                    self.prep_tile(gp + 1, t)

        def finish(self):
            pass

    class Scalar:
        def __init__(self, e):
            self.e = e

        def setup(self):
            e = self.e
            e.wait_ge(c_pool, 4)
            e.activation(identr[:], ident[:], ACT.Copy).then_inc(c_cst, 1)
            e.wait_ge(c_par, 1)
            e.activation(paramsT[:], pax[:, 0, 0:NC + 24], ACT.Copy).then_inc(c_parT, 1)
            e.activation(carry[:], half4[:, 0:1], ACT.Copy).then_inc(t_ex, CST)
            for t in range(T):
                self.keys_tile(0, t)

        def keys_tile(self, b, t):
            e, k = self.e, T * b + t
            e.wait_ge(k_max, 2 * k + 2)
            e.activation(keys[:, t, :], keys[:, t, :], ACT.Exp, bias=knm[:, t:t + 1],
                         accum_out=kz[:, t:t + 1]).then_inc(k_exp, 1)

        def search_alone(self, b):
            pass

        def boundary(self, ob, fb):
            e = self.e
            if ob is not None:
                self.out_rows(PAIRS * ob + PAIRS - 1, PAIRS - 1)
            if fb is not None:
                for g in range(2):
                    for t in range(4 * g, 4 * g + 4):
                        e.wait_ge(f_x1, T * fb + t + 1)
                        if g:
                            e.wait_ge(f_xt, 2 * KT * fb + KT)
                        e.activation(xr[:, t % 4, :], xin[:, t % 2, :], ACT.Square,
                                     accum_out=ssx[:, t:t + 1]).then_inc(f_sq, 1)
                    for k in range(KT):
                        wait_apart(e, f_xt, 2 * KT * fb + KT * g + k + 1, passed)
                        e.activation(xnT[:, k, g * HALF:(g + 1) * HALF], ppv[:, k % 2, :], ACT.Identity,
                                     scale=gain[:, k, bass.ds(fb, 1)],
                                     bias=gain[:, KT + k, bass.ds(fb, 1)]).then_inc(f_ev, 1)
            if ob is not None:
                for c in range(2):
                    e.wait_ge(d_y[c], 16 * T * (ob + 1))

        def prep_tile(self, gp, par, t):
            e, u = self.e, T * gp + t
            e.wait_ge(a_qkv, u + 1)
            e.activation(sq[:].rearrange("p h d -> p (h d)"), pax[:, 0, 0:4 * DH], ACT.Square).then_inc(a_sq, 1)
            e.activation(v2[:, par, t, :, 0:DH], pax[:, 0, 4 * DH:6 * DH].rearrange("p (h d) -> p h d", h=2),
                         ACT.Copy).then_inc(a_v, 1)

        def stack_tile(self, gp, par, t):
            e, u = self.e, T * gp + t
            e.wait_ge(a_tr, u + 1)
            e.activation(sB[par][:, :, t * P:(t + 1) * P], pax[:, 1, :].rearrange("p (h c) -> p h c", h=4),
                         ACT.Copy).then_inc(a_evB, 1)

        def max_row(self, gp, par, hh):
            e = self.e
            e.wait_ge(m_row, 2 * gp + hh + 1)
            e.activation(sA[par][DH:DH + 1, hh, :], pax[DH:DH + 1, :, :].rearrange("p a b -> p (a b)"),
                         ACT.Copy).then_inc(m_ev, 1)

        def exp(self, gp, hh, kt):
            e, w = self.e, T * (2 * gp + hh) + kt
            e.wait_ge(t_st, w + 1)
            e.wait_ge(t_pv, CST + w - 1)
            e.activation(pt[:, kt % 2, :], pst[:, 2 * (kt % 2):2 * (kt % 2) + 2, :].rearrange("p a b -> p (a b)"),
                         ACT.Exp, scale=DH ** -0.5).then_inc(t_ex, 1)

        def out_rows(self, gp, i):
            e = self.e
            for h in range(2):
                wait_apart(e, t_ot, 2 * gp + h + 1, passed)
                e.activation(oT[:, i, h * HALF:(h + 1) * HALF], pax[:, h, :], ACT.Copy).then_inc(t_oe, 1)

        def prep_alone(self, b, kb):
            gp = PAIRS * b
            for t in range(T):
                self.prep_tile(gp, 0, t)
                if kb is not None:
                    self.keys_tile(kb, t)
                if t > 0:
                    self.stack_tile(gp, 0, t - 1)
            self.stack_tile(gp, 0, T - 1)
            self.max_row(gp, 0, 0)

        def pair(self, b, i, par, search, prep, first):
            gp = PAIRS * b + i
            self.exp(gp, 0, 0)
            self.max_row(gp, par, 1)
            for t in range(T):
                if t < T - 1:
                    self.exp(gp, 0, t + 1)
                else:
                    self.exp(gp, 1, 0)
                if t == 0 and not first:
                    self.out_rows(gp - 1, i - 1)
                if prep:
                    self.prep_tile(gp + 1, 1 - par, t)
                    if t > 0:
                        self.stack_tile(gp + 1, 1 - par, t - 1)
            for t in range(T):
                if t < T - 1:
                    self.exp(gp, 1, t + 1)
                if prep and t == 0:
                    self.stack_tile(gp + 1, 1 - par, T - 1)
                if prep and t == 3:
                    self.max_row(gp + 1, 1 - par, 0)

        def finish(self):
            pass

    class Vector:
        def __init__(self, e):
            self.e = e

        def setup(self):
            e = self.e
            e.memset(mz[:].bitcast(F32), 0.0).then_inc(c_cst, 1)
            e.memset(cnt[:], 0.0).then_inc(z_cnt, CST)
            for t in range(T):
                self.keys_first(0, t)
                if t > 0:
                    self.keys_last(0, t - 1)
            self.keys_last(0, T - 1)
            e.wait_ge(c_cnd, 1)
            e.wait_ge(c_parT, 1)
            bias = paramsT[:, NC:NC + 16].unsqueeze(2).broadcast_to([P, 16, B])
            e.tensor_tensor(gain[:], pax[:, 1, 0:16 * B].rearrange("p (k b) -> p k b", b=B), bias,
                            ALU.add).then_inc(c_cndT, 1)
            e.wait_ge(c_cndT, 1)
            g = paramsT[:, NC + 16:NC + 24].unsqueeze(2).broadcast_to([P, KT, B])
            e.scalar_tensor_tensor(gain[:, 0:KT, :], gain[:, 0:KT, :], 1.0, g, ALU.add, ALU.mult).then_inc(c_cndT, 1)

        def keys_first(self, b, t):
            e, k, c = self.e, T * b + t, slice(t, t + 1)
            e.wait_ge(d_key[t], 16 * (b + 1))
            e.tensor_reduce(kmx[:, c], keys[:, t, :], axis=AX, op=ALU.max).then_inc(k_max, 1)
            e.wait_ge(k_max, 2 * k + 1)
            e.tensor_scalar(knm[:, c], kmx[:, c], -1.0, None, ALU.mult).then_inc(k_max, 1)

        def keys_last(self, b, t):
            e, k, c = self.e, T * b + t, slice(t, t + 1)
            e.wait_ge(k_exp, k + 1)
            e.reciprocal(krz[:, c], kz[:, c]).then_inc(k_key, 1)
            e.wait_ge(d_s, 16)
            e.wait_ge(k_key, 3 * k + 1)
            e.scalar_tensor_tensor(kw[:, c], krz[:, c], 1.0 / N ** 0.5, s_sb[:, bass.ds(b, 1), t], ALU.mult, ALU.mult).then_inc(k_key, 1)
            e.wait_ge(d_tb, 16 * (b + 1))
            e.wait_ge(k_key, 3 * k + 2)
            e.scalar_tensor_tensor(keys[:, t, :], tb[:], kw[:, c], keys[:, t, :], ALU.mult, ALU.mult).then_inc(k_key, 1)

        def search_init(self, b):
            e = self.e
            e.wait_ge(k_diag, T * (b + 1))
            e.memset(prefix[:], 0)
            e.memset(bit[:], SIGN)
            e.memset(cand[:], SIGN)
            e.memset(thr[:], 0).then_inc(z_init, 1)
            e.wait_ge(z_init, b + 1)

        def search_count(self, z, c):
            e = self.e
            kv = keys[:].rearrange("p t n -> p (t n)")[:, c * CHUNK:(c + 1) * CHUNK]
            e.wait_ge(z_cnt, CST + 4 * z + c - 1)
            e.tensor_scalar(trash[:, c % 2, :], kv, thr_f, None, ALU.is_ge, ALU.add,
                            accum_out=cnt[:, c:c + 1]).then_inc(z_cnt, 1)

        def search_update(self, z):
            e, n = self.e, 6 * z
            e.wait_ge(z_sum, z + 1)
            e.tensor_reduce(tot[:], tot4[:], axis=AX, op=ALU.add).then_inc(z_up, 1)
            e.wait_ge(z_up, n + 1)
            e.tensor_scalar(acc[:], tot[:], TOPK - 0.5, None, ALU.is_ge).then_inc(z_up, 1)
            e.wait_ge(z_up, n + 2)
            e.tensor_scalar(bit[:], bit[:], 1, None, ALU.logical_shift_right)
            e.copy_predicated(prefix[:], acc[:], cand[:]).then_inc(z_up, 1)
            e.wait_ge(z_up, n + 3)
            e.tensor_tensor(cand[:], prefix[:], bit[:], ALU.bitwise_or).then_inc(z_up, 1)
            e.wait_ge(z_up, n + 4)
            e.tensor_scalar(flip[:], cand[:], 31, -1, ALU.arith_shift_right, ALU.bitwise_xor).then_inc(z_up, 1)
            e.wait_ge(z_up, n + 5)
            e.scalar_tensor_tensor(thr[:], flip[:], SIGN, cand[:], ALU.bitwise_or, ALU.bitwise_xor).then_inc(z_up, 1)
            e.wait_ge(z_up, n + 6)

        def search_alone(self, b):
            self.search_init(b)
            with self.e.Fori(0, STEPS) as st:
                z = STEPS * b + st
                for c in range(4):
                    self.search_count(z, c)
                self.search_update(z)

        def boundary(self, ob, fb):
            e = self.e
            if ob is not None:
                e.wait_ge(d_wo, 16 * (ob + 1))
                for k in range(KT):
                    i = e.tensor_tensor(wo[:, k, k * P:(k + 1) * P], wo[:, k, k * P:(k + 1) * P], ident[:], ALU.add)
                i.then_inc(o_wi, 1)
            if fb is not None:
                n = F_STEPS * fb
                kv = keys[:].rearrange("p t n -> p (t n)")
                for j, op in enumerate((ALU.is_gt, ALU.is_equal)):
                    for c in range(4):
                        if 4 * j + c >= 2:
                            e.wait_ge(f_dve, n + 4 * j + c - 1)
                        e.tensor_scalar(trash[:, c % 2, :], kv[:, c * CHUNK:(c + 1) * CHUNK], thr_f, None, op, ALU.add,
                                        accum_out=cnt[:, 4 * j + c:4 * j + c + 1]).then_inc(f_dve, 1)
                e.wait_ge(f_sum, fb + 1)
                e.tensor_reduce(ngt[:], gt4[:], axis=AX, op=ALU.add).then_inc(f_dve, 1)
                e.wait_ge(f_tri, fb + 1)
                e.tensor_reduce(pre[:], ppv[:, 0, 0:4], axis=AX, op=ALU.add).then_inc(f_dve, 1)
                e.wait_ge(f_dve, n + 10)
                e.tensor_tensor(r0[:], ngt[:], pre[:], ALU.add).then_inc(f_dve, 1)
                e.wait_ge(f_dve, n + 11)
                e.tensor_scalar(rank[:], r0[:], -1.0, float(TOPK), ALU.mult, ALU.add).then_inc(f_dve, 1)
                e.wait_ge(f_dve, n + 12)
            for t in range(T):
                if fb is not None:
                    self.finalise_tile(fb, t)
                if ob is not None:
                    self.project_tile(ob, t)
            if fb is not None:
                for j in range(2):
                    e.wait_ge(d_x1[j], 16 * (T // 2) * (fb + 1))

        def finalise_tile(self, b, t):
            e, n = self.e, F_STEPS * b + 12 + 4 * t
            if t > 0:
                e.tensor_copy(carry[:], scn[:, N - 1:N]).then_inc(f_dve, 1)
            else:
                e.memset(carry[:], 0.0).then_inc(f_dve, 1)
            e.tensor_scalar(eqm[:], keys[:, t, :], thr_f, None, ALU.is_equal).then_inc(f_dve, 1)
            e.wait_ge(f_dve, n + 2)
            e.tensor_tensor_scan(scn[:], eqm[:], eqm[:], carry[:], ALU.add, ALU.max).then_inc(f_dve, 1)
            e.wait_ge(f_dve, n + 3)
            e.scalar_tensor_tensor(eqm[:], scn[:], rank[:], eqm[:], ALU.is_le, ALU.mult).then_inc(f_dve, 1)
            e.wait_ge(d_xin[t % 2], 16 * (T // 2 * b + t // 2 + 1))
            e.scalar_tensor_tensor(xin[:, t % 2, :], keys[:, t, :], thr_f, xin[:, t % 2, :],
                                   ALU.is_gt, ALU.add).then_inc(f_x1m, 1)
            e.wait_ge(f_dve, n + 4)
            e.wait_ge(f_x1m, T * b + t + 1)
            e.tensor_tensor(xin[:, t % 2, :], xin[:, t % 2, :], eqm[:], ALU.add).then_inc(f_x1, 1)
            e.wait_ge(f_rs, 2 * (T * b + t) + 2)
            e.tensor_scalar(xr[:, t % 4, :], xin[:, t % 2, :], rsx[:, t:t + 1], None, ALU.mult).then_inc(f_xr, 1)

        def project_tile(self, b, t):
            e = self.e
            for c in range(2):
                q = 2 * T * b + 2 * t + c
                e.wait_ge(o_mm, q + 1)
                e.wait_ge(d_res[c], 16 * (T * b + t + 1))
                if t > 0:
                    e.wait_ge(d_y[c], 16 * (T * b + t))
                cols = slice(c * HALF, (c + 1) * HALF)
                e.tensor_tensor(yout[:, cols], pst[:, (2 * t + c) % 4, :], xres[:, cols], ALU.add).then_inc(o_add, 1)

        def prep_tile(self, gp, par, t):
            e, u = self.e, T * gp + t
            e.wait_ge(a_sq, u + 1)
            e.tensor_reduce(ss[:], sq[:], axis=AX, op=ALU.add).then_inc(a_ss, 1)
            e.wait_ge(a_rs, 2 * u + 2)
            e.wait_ge(a_v, u + 1)
            for h in range(4):
                i = e.scalar_tensor_tensor(qkn[:, h, :], pax[:, 0, h * DH:(h + 1) * DH], rs[:, h:h + 1],
                                           gqk[:, h // 2, :], ALU.mult, ALU.mult)
            i.then_inc(a_nm, 1)
            wait(e, a_tr, u - 1)
            e.wait_ge(a_nm, 3 * u + 1)
            st = stage[:, t % 2, :, :]
            e.tensor_copy(st[:, 0:2, 0:DH], qkn[:, 0:2, :])
            e.tensor_copy(st[:, 2:4, DH:P], qkn[:, 2:4, :]).then_inc(a_nm, 1)
            e.wait_ge(a_nm, 3 * u + 2)
            e.tensor_tensor(st[:, 0:2, DH:P], qkn[:, 0:2, :], st[:, 0:2, 0:DH].bitcast(F32), ALU.subtract)
            e.tensor_tensor(st[:, 2:4, 0:DH], qkn[:, 2:4, :], st[:, 2:4, DH:P].bitcast(F32),
                            ALU.subtract).then_inc(a_nm, 1)

        def stack_tile(self, gp, par, t):
            e, u = self.e, T * gp + t
            e.wait_ge(a_evB, u + 1)
            src = pax[:, 1, :].rearrange("p (h c) -> p h c", h=4)
            cols = slice(t * P, (t + 1) * P)
            e.tensor_copy(sA[par][0:DH, 2:4, cols], src[DH:P, 2:4, :])
            e.tensor_copy(sA[par][0:DH, 0:2, cols], src[0:DH, 0:2, :]).then_inc(a_evA, 1)

        def row_max(self, gp, j):
            e, v = self.e, 2 * T * gp + j
            e.wait_ge(m_s, v + 1)
            e.tensor_reduce(mz[:, j // T, DH + j % T:DH + j % T + 1], pax[:].rearrange("p a b -> p (a b)"),
                            axis=AX, op=ALU.max).then_inc(m_mx, 1)

        def normalise(self, gp, hh):
            e, g = self.e, 2 * gp + hh
            e.wait_ge(t_pv, CST + T * (g + 1))
            ov = ppv[:, :, 0:4 * (DH + 1)].rearrange("p a (q d) -> p a q d", q=4)
            rv = rl[:].rearrange("p (a q) -> p a q", a=2)
            e.reciprocal(rv, ov[:, :, :, DH]).then_inc(t_rl, 1)
            e.wait_ge(t_rl, g + 1)
            for a in range(2):
                i = e.tensor_tensor(otok[:, 4 * a:4 * a + 4, hh * DH:(hh + 1) * DH], ov[:, a, :, 0:DH],
                                    rv[:, a, :].unsqueeze(2).broadcast_to([P, 4, DH]), ALU.mult)
            i.then_inc(t_on, 1)

        def prep_alone(self, b, kb):
            gp = PAIRS * b
            for t in range(T):
                if kb is not None:
                    self.keys_first(kb, t)
                self.prep_tile(gp, 0, t)
                if kb is not None:
                    self.keys_last(kb, t)
                if t > 0:
                    self.stack_tile(gp, 0, t - 1)
            self.stack_tile(gp, 0, T - 1)
            for j in range(2 * T):
                self.row_max(gp, j)

        def pair(self, b, i, par, search, prep, first):
            gp = PAIRS * b + i
            if search and first:
                self.search_init(b + 1)
            for t in range(T):
                if search:
                    z = STEPS * (b + 1) + 4 * i + t // 2
                    for c in (0, 1):
                        self.search_count(z, 2 * (t % 2) + c)
                if prep:
                    self.prep_tile(gp + 1, 1 - par, t)
                    if t > 0:
                        self.stack_tile(gp + 1, 1 - par, t - 1)
                if search and t % 2 == 1:
                    self.search_update(z)
            self.normalise(gp, 0)
            if prep:
                self.stack_tile(gp + 1, 1 - par, T - 1)
                for j in range(2 * T):
                    self.row_max(gp + 1, j)
            self.normalise(gp, 1)

        def finish(self):
            pass

    class Tensor:
        def __init__(self, e):
            self.e = e

        def setup(self):
            e = self.e
            e.wait_ge(d_par, 48)
            e.wait_ge(c_pool, 4)
            e.transpose(pax[:, 0, 0:NC + 24], params[:], ident[0:NC + 24, 0:NC + 24]).then_inc(c_par, 1)
            e.wait_ge(c_parT, 1)
            e.wait_ge(d_wemb, 16)
            ct = paramsT[:, 0:NC].rearrange("p (b k) -> p k b", k=KT)
            for j in range(2 * KT):
                for k in range(KT):
                    i = e.matmul(pax[:, 1, j * B:(j + 1) * B], wemb_v[:, k, j * P:(j + 1) * P], ct[:, k, 0:B],
                                 start=(k == 0), stop=(k == KT - 1))
            i.then_inc(c_cnd, 1)
            e.wait_ge(c_cst, 2)
            e.matmul(ppv[:, 1, 0:P], ident[:], ident[:], start=True, stop=True).then_inc(t_pv, CST)

        def search_alone(self, b):
            pass

        def boundary(self, ob, fb):
            e = self.e
            if ob is not None:
                self.out_rows(PAIRS * ob + PAIRS - 1)
                e.wait_ge(t_oe, 2 * PAIRS * (ob + 1))
                e.wait_ge(o_wi, ob + 1)
                e.wait_ge(t_on, 2 * PAIRS * (ob + 1))
            for t in range(T):
                if ob is not None:
                    self.project_tile(ob, t, 0)
                if fb is not None and t == 0:
                    self.before(fb)
                if ob is not None:
                    self.project_tile(ob, t, 1)
                if fb is not None and t % 4 == 3:
                    self.features(fb, t // 4)

        def before(self, b):
            e = self.e
            e.wait_ge(f_dve, F_STEPS * b + 8)
            e.matmul(ppv[:, 0, 0:4], tri[:], cnt[:, 4:8], start=True, stop=True).then_inc(f_tri, 1)

        def features(self, b, g):
            e = self.e
            e.wait_ge(f_xr, T * b + 4 * g + 4)
            for k in range(KT):
                n = 2 * KT * b + KT * g + k
                if k > 1 or g:
                    e.wait_ge(f_ev, n - 1)
                for j in range(4):
                    i = e.transpose(ppv[:, k % 2, j * P:(j + 1) * P], xr[:, j, k * P:(k + 1) * P], ident[:])
                i.then_inc(f_xt, 1)

        def project_tile(self, b, t, c):
            e, q = self.e, 2 * T * b + 2 * t + c
            if 2 * t + c >= 4:
                e.wait_ge(o_add, q - 3)
            for k in range(KT):
                i = e.matmul(pst[:, (2 * t + c) % 4, :], oT[:, k, t * P:(t + 1) * P],
                             wo[:, k, c * HALF:(c + 1) * HALF], start=(k == 0), stop=(k == KT - 1))
            i.then_inc(o_mm, 1)

        def prep_tile(self, gp, t):
            e, u = self.e, T * gp + t
            if t == 0:
                e.wait_ge(d_w, 48 * (gp + 1))
            else:
                e.wait_ge(a_nm, 3 * u - 2)
                e.wait_ge(a_v, u)
            for k in range(KT):
                i = e.matmul(pax[:, 0, 0:6 * DH], xnT[:, k, t * P:(t + 1) * P],
                             wq[:, k, :, :].rearrange("p s c -> p (s c)"), start=(k == 0), stop=(k == KT - 1))
            i.then_inc(a_qkv, 1)

        def transpose_tile(self, gp, t):
            e, u = self.e, T * gp + t
            e.wait_ge(a_nm, 3 * u + 3)
            if t > 0:
                e.wait_ge(a_evA, u)
                e.wait_ge(a_evB, u)
            for h in range(4):
                i = e.transpose(paxr[:, 1, h * P:(h + 1) * P], stage[:, t % 2, h, :], identr[:])
            i.then_inc(a_tr, 1)

        def score_max(self, gp, par, j):
            e, v = self.e, 2 * T * gp + j
            if j == 0:
                e.wait_ge(a_evA, T * (gp + 1))
                e.wait_ge(a_evB, T * (gp + 1))
                e.wait_ge(a_row, 2 * (gp + 1))
            elif j == T:
                e.wait_ge(m_ev, 2 * gp + 1)
            else:
                e.wait_ge(m_mx, v)
            hh, qt = j // T, j % T
            for c in range(2):
                i = e.matmul(pax[:, c, :], sA[par][0:DH + 1, hh, qt * P:(qt + 1) * P],
                             sA[par][0:DH + 1, 2 + hh, c * HALF:(c + 1) * HALF], start=True, stop=True)
            i.then_inc(m_s, 1)

        def max_row(self, gp, hh):
            e = self.e
            e.wait_ge(m_mx, 2 * T * gp + T * (hh + 1))
            for q in range(T):
                i = e.matmul(pax[0:DH + 1, q // 4, (q % 4) * P:(q % 4 + 1) * P], mz[:, hh, q:q + DH + 1],
                             identr[:], start=True, stop=True)
            i.then_inc(m_row, 1)

        def scores(self, gp, par, hh, kt):
            e, w = self.e, T * (2 * gp + hh) + kt
            if kt == 0:
                e.wait_ge(m_ev, 2 * gp + hh + 1)
            e.wait_ge(t_ex, CST + w - 1)
            for m, (op, k) in enumerate(((sA[par], DH + 1), (sB[par], P))):
                for c in range(2):
                    i = e.matmul(pst[:, 2 * (kt % 2) + c, :], op[0:k, 2 + hh, kt * P:(kt + 1) * P],
                                 op[0:k, hh, c * HALF:(c + 1) * HALF], start=(m == 0), stop=(m == 1),
                                 skip_group_check=True)
            i.then_inc(t_st, 1)

        def values(self, gp, par, hh, kt):
            e, w = self.e, T * (2 * gp + hh) + kt
            if kt == 0:
                wait(e, t_on, 2 * gp + hh if isinstance(gp, int) or hh else 2 * gp)
            e.wait_ge(t_ex, CST + w + 1)
            for q in range(T):
                c = (q % 4) * (DH + 1)
                i = e.matmul(ppv[:, q // 4, c:c + DH + 1], pt[:, kt % 2, q * P:(q + 1) * P],
                             v2[:, par, kt, hh, :], start=(kt == 0 and q % 4 == 0), stop=(kt == T - 1),
                             skip_group_check=True)
            i.then_inc(t_pv, 1)

        def out_rows(self, gp):
            e = self.e
            e.wait_ge(t_on, 2 * gp + 2)
            for t in range(T):
                i = e.transpose(pax[:, t // 4, (t % 4) * P:(t % 4 + 1) * P], otok[:, t, :], ident[:])
                if t % 4 == 3:
                    i.then_inc(t_ot, 1)

        def prep_alone(self, b, kb):
            e, gp = self.e, PAIRS * b
            wait(e, t_oe, 2 * gp)
            e.wait_ge(f_ev, 2 * KT * (b + 1))
            if isinstance(gp, int) and gp == 0:
                e.wait_ge(c_cndT, 2)
                e.wait_ge(d_gqk, 32)
            for t in range(T):
                self.prep_tile(gp, t)
                if t > 0:
                    self.transpose_tile(gp, t - 1)
            self.transpose_tile(gp, T - 1)
            for j in range(T):
                self.score_max(gp, 0, j)
            self.max_row(gp, 0)
            for j in range(T, 2 * T):
                self.score_max(gp, 0, j)

        def pair(self, b, i, par, search, prep, first):
            e, gp = self.e, PAIRS * b + i
            self.scores(gp, par, 0, 0)
            self.max_row(gp, 1)
            for t in range(T):
                if t < T - 1:
                    self.scores(gp, par, 0, t + 1)
                else:
                    self.scores(gp, par, 1, 0)
                if t == 0:
                    e.wait_ge(m_ev, 2 * gp + 2)
                    if not first:
                        self.out_rows(gp - 1)
                self.values(gp, par, 0, t)
                if t == 0 and not first:
                    e.wait_ge(t_oe, 2 * gp)
                if prep:
                    self.prep_tile(gp + 1, t)
                    if t > 0:
                        self.transpose_tile(gp + 1, t - 1)
            for t in range(T):
                if t < T - 1:
                    self.scores(gp, par, 1, t + 1)
                if prep and t == 0:
                    self.transpose_tile(gp + 1, T - 1)
                if prep and t > 0:
                    self.score_max(gp + 1, 1 - par, 2 * t)
                self.values(gp, par, 1, t)
                if prep and t == 0:
                    self.score_max(gp + 1, 1 - par, 0)
                if prep:
                    self.score_max(gp + 1, 1 - par, 2 * t + 1)
                if prep and t == 3:
                    self.max_row(gp + 1, 0)

        def finish(self):
            pass

    F_STEPS = 12 + 4 * T
    f_x1m = sem("f_x1m")

    def batch(s, b, search, fb, kb):
        s.pair(b, 0, 0, search, True, True)
        with s.e.Fori(0, (PAIRS - 2) // 2) as ii:
            s.pair(b, 2 * ii + 1, 1, search, True, False)
            s.pair(b, 2 * ii + 2, 0, search, True, False)
        s.pair(b, PAIRS - 1, 1, search, False, False)
        s.boundary(b, fb)
        if fb is not None:
            s.prep_alone(fb, kb)

    def program(s):
        s.setup()
        s.search_alone(0)
        s.boundary(None, 0)
        s.prep_alone(0, 1 if B > 1 else None)
        if B > 2:
            with s.e.Fori(0, B - 2) as b:
                batch(s, b, True, b + 1, b + 2)
        if B > 1:
            batch(s, B - 2, True, B - 1, None)
        batch(s, B - 1, False, None, None)
        s.finish()

    with nc.Block() as block:
        @block.sync
        def _(e):
            program(Sync(e))

        @block.gpsimd
        def _(e):
            program(Pool(e))

        @block.scalar
        def _(e):
            program(Scalar(e))

        @block.vector
        def _(e):
            program(Vector(e))

        @block.tensor
        def _(e):
            program(Tensor(e))


NAMES = ["x", "fside_BxSx1_0", "cond_2048", "L1_cond_W_emb", "L1_cond_b_emb", "L1_cond_g_norm",
         "L1_cond_W_qkv", "L1_cond_g_q", "L1_cond_g_k", "L1_cond_W_out"]


def kernel(**inputs):
    import numpy as np
    import concourse.bacc as bacc
    from concourse.bass_utils import run_bass_kernel_spmd

    nc = bacc.Bacc("TRN2", target_bir_lowering=False, num_devices=1)
    arrays, args = {}, []
    for name in NAMES:
        a = np.ascontiguousarray(inputs[name])
        arrays[f"in_{name}"] = a
        args.append(nc.dram_tensor(f"in_{name}", a.shape, mybir.dt.from_np(a.dtype), kind="ExternalInput").ap())
    args.append(nc.dram_tensor("out_x", arrays["in_x"].shape, F32, kind="ExternalOutput").ap())
    with ExitStack() as ctx:
        cond_block(nc, *args, ctx)
    r = run_bass_kernel_spmd(nc, [arrays], core_ids=[0])
    return r.results[0]["out_x"]
```

```python
from contextlib import ExitStack

import concourse.bass as bass
from concourse import mybir

F32 = mybir.dt.float32
F32R = mybir.dt.float32r
I32 = mybir.dt.int32
U8 = mybir.dt.uint8
ALU = mybir.AluOpType
ACT = mybir.ActivationFunctionType
AX = mybir.AxisListType.X
ADD_ALL = bass.bass_isa.ReduceOp.add
P = 128
LOWEST = -3.4028234663852886e38
SIGN = -2147483648


def wait(e, sem, value):
    if not isinstance(value, int) or value > 0:
        e.wait_ge(sem, value)


def wait_apart(e, sem, value, passed):
    e.wait_ge(sem, value)
    e.sem_inc(passed, 1)


def cond_block(nc, x, s_in, cond, w_emb, b_emb, g_norm, w_qkv, g_q, g_k, w_out, out, ctx):
    B, N, D = x.shape
    T = N // P
    KT = D // P
    DH = g_q.shape[0]
    HEADS = D // DH
    PAIRS = HEADS // 2
    TOPK = 10240
    STEPS = 32
    EPS = 1e-6
    HALF = N // 2
    CHUNK = T * N // 4
    NC = B * KT
    assert T == 8 and KT == 8 and PAIRS == 8 and HALF == 512 and DH == 64

    def sem(name):
        return ctx.enter_context(nc.semaphore(name))

    def sb(name, shape, dt=F32):
        return ctx.enter_context(nc.sbuf_tensor(name, shape, dt))

    keys = sb("keys", [P, T, N])
    feat = sb("feat", [P, 2 * KT, N])
    xnT, oT = feat[:, 0:KT, :], feat[:, KT:2 * KT, :]
    wemb_v = feat[:].rearrange("p k n -> p (k n)").rearrange("p (k n) -> p k n", k=KT)
    wq = sb("wq", [P, KT, 3, P])
    v2 = sb("v2", [P, 2, T, 2, DH + 1])
    pt = sb("pt", [P, 2, N])
    stage = sb("stage", [P, 4, P], F32R)
    sq = sb("sq", [P, 4, DH])
    qkn = sb("qkn", [P, 4, DH])
    otok = sb("otok", [P, T, P])
    trash = sb("trash", [P, 2, CHUNK], U8)
    gqk = sb("gqk", [P, 2, DH])
    identr = sb("identr", [P, P], F32R)
    ident = identr[:].bitcast(F32)
    heads_t = sb("heads_t", [DH + 1, N])
    tri = sb("tri", [P, P])
    mz = sb("mz", [P, 2, DH + T], F32R)
    mx2 = sb("mx2", [P, 2, T, 2])
    paramsT = sb("paramsT", [P, NC + 24])
    gain = sb("gain", [P, 2 * KT, B])
    s_sb = sb("s_sb", [P, B, T])
    small = {n: sb(n, [P, w]) for n, w in dict(
        ss=4, rs=4, half4=4, rl=T, kmx=T, knm=T, kz=T, krz=T, kw=T, cnt=8, tot4=4, tot=1, gt4=4, ngt=1,
        pre=1, r0=1, rank=1, carry=1, ssx=T, rsx=T).items()}
    ss, rs, half4, rl = (small[n] for n in ("ss", "rs", "half4", "rl"))
    kmx, knm, kz, krz, kw = (small[n] for n in ("kmx", "knm", "kz", "krz", "kw"))
    cnt, tot4, tot, gt4, ngt, pre, r0, rank, carry, ssx, rsx = (
        small[n] for n in ("cnt", "tot4", "tot", "gt4", "ngt", "pre", "r0", "rank", "carry", "ssx", "rsx"))
    prefix, bit, cand, flip, thr, acc = (sb(n, [P, 1], I32) for n in ("prefix", "bit", "cand", "flip", "thr", "acc"))
    thr_f = thr[:].bitcast(F32)
    inner = ExitStack()
    sB0 = inner.enter_context(nc.sbuf_tensor("sB0", [P, 4, N], F32R))
    sA0 = inner.enter_context(nc.sbuf_tensor("sA0", [P, 4, N], F32R))
    sB1 = inner.enter_context(nc.sbuf_tensor("sB1", [P, 4, N], F32R))
    sA1 = inner.enter_context(nc.sbuf_tensor("sA1", [P, 4, N], F32R))
    inner.close()
    sA, sB = [sA0, sA1], [sB0, sB1]
    wo = sb("wo", [P, KT, N])
    xin = sb("xin", [P, 2, N])
    xr = sb("xr", [P, 4, N])
    eqm = sb("eqm", [P, N])
    scn = sb("scn", [P, N])
    params = scn[0:NC + 24, 0:P]
    tb = eqm
    xres, yout = pt[:, 0, :], pt[:, 1, :]

    pst = ctx.enter_context(nc.psum_tensor("pst", [P, 4, HALF], F32))
    ppv = ctx.enter_context(nc.psum_tensor("ppv", [P, 2, HALF], F32))
    pax = ctx.enter_context(nc.psum_tensor("pax", [P, 2, HALF], F32))
    paxr = pax[:].bitcast(F32R)

    d_par, d_wemb, d_gqk, d_s, d_tb, d_w, d_wo = (sem(n) for n in ("d_par", "d_wemb", "d_gqk", "d_s", "d_tb", "d_w", "d_wo"))
    d_key = [sem(f"d_key{t}") for t in range(T)]
    d_xin = [sem(f"d_xin{t}") for t in range(2)]
    d_x1 = [sem(f"d_x1{t}") for t in range(2)]
    d_res = [sem(f"d_res{t}") for t in range(2)]
    d_y = [sem(f"d_y{t}") for t in range(2)]
    c_pool, c_cst, c_par, c_parT, c_cnd, c_cndT = (sem(n) for n in ("c_pool", "c_cst", "c_par", "c_parT", "c_cnd", "c_cndT"))
    k_max, k_key, k_exp, k_diag = sem("k_max"), sem("k_key"), sem("k_exp"), sem("k_diag")
    passed = sem("passed")
    z_init, z_cnt, z_sum, z_up = sem("z_init"), sem("z_cnt"), sem("z_sum"), sem("z_up")
    f_dve, f_sum, f_tri, f_x1, f_sq, f_rs, f_xr, f_xt, f_ev = (
        sem(n) for n in ("f_dve", "f_sum", "f_tri", "f_x1", "f_sq", "f_rs", "f_xr", "f_xt", "f_ev"))
    a_qkv, a_sq, a_v, a_ss, a_rs, a_nm, a_tr, a_ev, a_row = (
        sem(n) for n in ("a_qkv", "a_sq", "a_v", "a_ss", "a_rs", "a_nm", "a_tr", "a_ev", "a_row"))
    m_s, m_mx, m_cb, m_row, m_ev = (sem(n) for n in ("m_s", "m_mx", "m_cb", "m_row", "m_ev"))
    t_st, t_ex, t_pv, t_mv, t_tk, t_rl, t_on, t_ot, t_oe = (sem(n) for n in ("t_st", "t_ex", "t_pv", "t_mv", "t_tk", "t_rl", "t_on", "t_ot", "t_oe"))
    o_wi, o_mm, o_add = sem("o_wi"), sem("o_mm"), sem("o_add")

    x_v = x.rearrange("b (p t) n -> b p t n", t=T)
    out_v = out.rearrange("b (p t) n -> b p t n", t=T)
    wqkv_v = w_qkv.rearrange("(k p) (s i c) -> p k s i c", p=P, s=3, i=PAIRS)

    def qkv_bank(alone, t):
        return ppv[:, 0, :] if alone and t % 2 else pax[:, 0, :]

    def max_banks(alone, j):
        return ppv if alone and (j + j // T) % 2 else pax

    CST = 2

    class Sync:
        def __init__(self, e):
            self.e = e

        def setup(self):
            e = self.e
            self.load_keys(0)
            e.dma_start(params[0:NC, :], cond.rearrange("b (k p) -> (b k) p", p=P)).then_inc(d_par, 16)
            e.dma_start(params[NC:NC + 16, :], b_emb.rearrange("(k p) -> k p", p=P)).then_inc(d_par, 16)
            e.dma_start(params[NC + 16:NC + 24, :], g_norm.rearrange("(k p) -> k p", p=P)).then_inc(d_par, 16)
            e.dma_start(s_sb[:], s_in.rearrange("b (p t) a -> p b (t a)", t=T)).then_inc(d_s, 16)
            e.dma_start(gqk[:, 0, :], g_q.partition_broadcast(P)).then_inc(d_gqk, 16)
            e.dma_start(gqk[:, 1, :], g_k.partition_broadcast(P)).then_inc(d_gqk, 16)
            e.dma_start(wemb_v, w_emb.rearrange("(k p) n -> p k n", p=P)).then_inc(d_wemb, 16)
            self.load_w(0)

        def load_keys(self, b):
            e = self.e
            for t in range(T):
                e.dma_start(keys[:, t, :], x_v[b, :, t, :]).then_inc(d_key[t], 16)
            e.dma_start(tb[:], cond[b, :].partition_broadcast(P)).then_inc(d_tb, 16)

        def load_w(self, i):
            for s in range(3):
                self.e.dma_start(wq[:, :, s, :], wqkv_v[:, :, s, i, :]).then_inc(d_w, 16)

        def search_alone(self, b):
            pass

        def x_tile(self, b, t):
            self.e.dma_start(xin[:, t % 2, :], x_v[b, :, t, :]).then_inc(d_xin[t % 2], 16)

        def finalise_tile(self, b, t):
            e = self.e
            e.wait_ge(f_x1, T * b + t + 1)
            e.dma_start(out_v[b, :, t, :], xin[:, t % 2, :]).then_inc(d_x1[t % 2], 16)
            if t + 2 < T:
                e.wait_ge(d_x1[t % 2], 16 * (T // 2 * b + t // 2 + 1))
                e.wait_ge(f_xr, T * b + t + 1)
                self.x_tile(b, t + 2)

        def boundary(self, ob, fb):
            e = self.e
            if ob is not None:
                wait_apart(e, t_pv, CST + T * 2 * PAIRS * (ob + 1), passed)
                for j in range(2):
                    e.wait_ge(d_x1[j], 16 * (T // 2) * (ob + 1))
                for c in range(2):
                    self.residual(ob, 0, c)
            if fb is not None:
                self.x_tile(fb, 0)
                self.x_tile(fb, 1)
            for t in range(T):
                if fb is not None:
                    self.finalise_tile(fb, t)
                if ob is not None:
                    for c in range(2):
                        e.wait_ge(o_add, 2 * T * ob + 2 * t + c + 1)
                        e.dma_start(out_v[ob, :, t, c * HALF:(c + 1) * HALF],
                                    yout[:, c * HALF:(c + 1) * HALF]).then_inc(d_y[c], 16)
                        if t + 1 < T:
                            self.residual(ob, t + 1, c)

        def residual(self, b, t, c):
            self.e.dma_start(xres[:, c * HALF:(c + 1) * HALF],
                             out_v[b, :, t, c * HALF:(c + 1) * HALF]).then_inc(d_res[c], 16)

        def prep_alone(self, b, kb):
            e = self.e
            if kb is not None:
                e.wait_ge(f_xr, T * (b + 1))
                self.load_keys(kb)
            e.wait_ge(a_qkv, T * (PAIRS * b + 1))
            self.load_w(1)

        def pair(self, b, i, par, search, prep, first):
            e, gp = self.e, PAIRS * b + i
            if prep:
                wait_apart(e, a_qkv, T * (gp + 2), passed)
                self.load_w((i + 2) % PAIRS)
            else:
                e.wait_ge(t_pv, CST + 2 * T * gp)
                e.dma_start(wo[:], w_out.rearrange("(k p) n -> p k n", p=P)).then_inc(d_wo, 16)

        def finish(self):
            for c in range(2):
                self.e.wait_ge(d_y[c], 16 * T * B)
                self.e.wait_ge(d_x1[c], 16 * T // 2 * B)

    class Pool:
        def __init__(self, e):
            self.e = e

        def setup(self):
            e = self.e
            e.memset(scn[:, P:2 * P], 0.0).then_inc(c_pool, 1)
            e.memset(tri[:], 1.0).then_inc(c_pool, 1)
            e.memset(half4[:], -0.5).then_inc(c_pool, 1)
            e.wait_ge(c_pool, 3)
            e.affine_select(out=identr[:], in_=scn[:, P:2 * P], compare_op=ALU.not_equal, fill=1.0, base=0,
                            pattern=[[-1, P]], channel_multiplier=1).then_inc(c_pool, 1)
            e.affine_select(out=tri[:], in_=tri[:], compare_op=ALU.is_gt, fill=0.0, base=0,
                            pattern=[[1, P]], channel_multiplier=-1).then_inc(c_pool, 1)
            e.memset(v2[:, :, :, :, DH:DH + 1], 1.0).then_inc(c_pool, 1)
            for t in range(T):
                self.keys_tile(0, t)

        def keys_tile(self, b, t):
            e, k = self.e, T * b + t
            wait_apart(e, k_key, 3 * k + 3, passed)
            e.affine_select(out=keys[:, t, :], in_=keys[:, t, :], compare_op=ALU.not_equal, fill=LOWEST,
                            base=t, pattern=[[-1, N]], channel_multiplier=T).then_inc(k_diag, 1)
            wait_apart(e, k_diag, k + 1, passed)

        def search_alone(self, b):
            with self.e.Fori(0, STEPS) as st:
                self.search_sum(STEPS * b + st)

        def search_sum(self, z):
            e = self.e
            wait_apart(e, z_cnt, CST + 4 * z + 4, passed)
            e.partition_all_reduce(tot4[:], cnt[:, 0:4], P, ADD_ALL).then_inc(z_sum, 1)

        def boundary(self, ob, fb):
            if fb is None:
                return
            e = self.e
            wait_apart(e, f_dve, F_STEPS * fb + 4, passed)
            e.partition_all_reduce(gt4[:], cnt[:, 0:4], P, ADD_ALL).then_inc(f_sum, 1)
            for t in range(T):
                n = T * fb + t
                wait_apart(e, f_sq, n + 1, passed)
                e.tensor_scalar(rsx[:, t:t + 1], ssx[:, t:t + 1], 1.0 / D, EPS, ALU.mult, ALU.add).then_inc(f_rs, 1)
                e.wait_ge(f_rs, 2 * n + 1)
                e.tensor_tensor(rsx[:, t:t + 1], rsx[:, t:t + 1], half4[:, 0:1], ALU.pow).then_inc(f_rs, 1)

        def prep_tile(self, gp, t):
            e, u = self.e, T * gp + t
            wait_apart(e, a_ss, u + 1, passed)
            e.tensor_scalar(rs[:], ss[:], 1.0 / DH, EPS, ALU.mult, ALU.add).then_inc(a_rs, 1)
            e.wait_ge(a_rs, 2 * u + 1)
            e.tensor_tensor(rs[:], rs[:], half4[:], ALU.pow).then_inc(a_rs, 1)

        def prep_rows(self, gp, par):
            e = self.e
            wait_apart(e, a_qkv, T * gp + 1, passed)
            e.memset(sA[par][DH:DH + 1, 0:2, :].bitcast(F32), 0.0).then_inc(a_row, 1)
            e.memset(sA[par][DH:DH + 1, 2:4, :].bitcast(F32), -1.0).then_inc(a_row, 1)
            wait_apart(e, a_row, 2 * (gp + 1), passed)

        def prep_alone(self, b, kb):
            gp = PAIRS * b
            self.prep_rows(gp, 0)
            for t in range(T):
                self.prep_tile(gp, t)
                if kb is not None and t > 0:
                    self.keys_tile(kb, t - 1)
            if kb is not None:
                self.keys_tile(kb, T - 1)

        def pair(self, b, i, par, search, prep, first):
            gp = PAIRS * b + i
            if prep:
                self.prep_rows(gp + 1, 1 - par)
            for t in range(T):
                last = prep and t == T - 1
                if search and t % 2 == 1 and not last:
                    self.search_sum(STEPS * (b + 1) + 4 * i + t // 2)
                if prep:
                    self.prep_tile(gp + 1, t)
                if search and last:
                    self.search_sum(STEPS * (b + 1) + 4 * i + t // 2)

        def finish(self):
            pass

    class Scalar:
        def __init__(self, e):
            self.e = e

        def setup(self):
            e = self.e
            e.wait_ge(c_par, 1)
            e.activation(paramsT[:], pax[:, 0, 0:NC + 24], ACT.Copy).then_inc(c_parT, 1)
            e.activation(carry[:], half4[:, 0:1], ACT.Copy).then_inc(t_ex, CST)
            for t in range(T):
                self.keys_tile(0, t)

        def keys_tile(self, b, t):
            e, k = self.e, T * b + t
            e.wait_ge(k_max, 2 * k + 2)
            e.activation(keys[:, t, :], keys[:, t, :], ACT.Exp, bias=knm[:, t:t + 1],
                         accum_out=kz[:, t:t + 1]).then_inc(k_exp, 1)

        def search_alone(self, b):
            pass

        def boundary(self, ob, fb):
            e = self.e
            if ob is not None:
                for h in range(2):
                    self.out_rows(PAIRS * ob + PAIRS - 1, PAIRS - 1, h)
            if fb is not None:
                for g in range(2):
                    for t in range(4 * g, 4 * g + 4):
                        e.wait_ge(f_x1, T * fb + t + 1)
                        if g:
                            e.wait_ge(f_xt, 2 * KT * fb + KT)
                        e.activation(xr[:, t % 4, :], xin[:, t % 2, :], ACT.Square,
                                     accum_out=ssx[:, t:t + 1]).then_inc(f_sq, 1)
                    for k in range(KT):
                        wait_apart(e, f_xt, 2 * KT * fb + KT * g + k + 1, passed)
                        e.activation(xnT[:, k, g * HALF:(g + 1) * HALF], ppv[:, k % 2, :], ACT.Identity,
                                     scale=gain[:, k, bass.ds(fb, 1)],
                                     bias=gain[:, KT + k, bass.ds(fb, 1)]).then_inc(f_ev, 1)
            if ob is not None:
                for c in range(2):
                    e.wait_ge(d_y[c], 16 * T * (ob + 1))

        def prep_tile(self, gp, par, t, alone=False):
            e, u = self.e, T * gp + t
            bank = qkv_bank(alone, t)
            e.wait_ge(a_qkv, u + 1)
            wait(e, a_nm, 3 * u)
            e.activation(qkn[:].rearrange("p h d -> p (h d)"), bank[:, 0:4 * DH], ACT.Copy)
            e.activation(sq[:].rearrange("p h d -> p (h d)"), bank[:, 0:4 * DH], ACT.Square).then_inc(a_sq, 1)
            e.activation(v2[:, par, t, :, 0:DH], bank[:, 4 * DH:6 * DH].rearrange("p (h d) -> p h d", h=2),
                         ACT.Copy).then_inc(a_v, 1)

        def stack_tile(self, gp, par, t):
            e, u = self.e, T * gp + t
            e.wait_ge(a_tr, u + 1)
            src = pax[:, 1, :].rearrange("p (h c) -> p h c", h=4)
            cols = slice(t * P, (t + 1) * P)
            e.activation(sB[par][:, :, cols], src, ACT.Copy)
            e.activation(sA[par][0:DH, 2:4, cols], src[DH:P, 2:4, :], ACT.Copy)
            e.activation(sA[par][0:DH, 0:2, cols], src[0:DH, 0:2, :], ACT.Copy).then_inc(a_ev, 1)

        def max_row(self, gp, par, hh):
            e = self.e
            e.wait_ge(m_row, 2 * gp + hh + 1)
            e.activation(sA[par][DH:DH + 1, hh, :], pax[DH:DH + 1, :, :].rearrange("p a b -> p (a b)"),
                         ACT.Copy).then_inc(m_ev, 1)

        def exp(self, gp, hh, kt):
            e, w = self.e, T * (2 * gp + hh) + kt
            e.wait_ge(t_st, w + 1)
            e.wait_ge(t_pv, CST + w - 1)
            e.activation(pt[:, kt % 2, :], pst[:, 2 * (kt % 2):2 * (kt % 2) + 2, :].rearrange("p a b -> p (a b)"),
                         ACT.Exp, scale=DH ** -0.5).then_inc(t_ex, 1)

        def out_move(self, gp, hh):
            e, g = self.e, 2 * gp + hh
            e.wait_ge(t_pv, CST + T * (g + 1))
            e.activation(heads_t[:], ppv[0:DH + 1, :, :].rearrange("p a b -> p (a b)"), ACT.Copy).then_inc(t_mv, 1)

        def out_rows(self, gp, i, h):
            e = self.e
            wait_apart(e, t_ot, 2 * gp + h + 1, passed)
            e.activation(oT[:, i, h * HALF:(h + 1) * HALF], pax[:, 1, :], ACT.Copy).then_inc(t_oe, 1)

        def prep_alone(self, b, kb):
            gp = PAIRS * b
            for t in range(T):
                self.prep_tile(gp, 0, t, True)
                if kb is not None:
                    self.keys_tile(kb, t)
                if t > 0:
                    self.stack_tile(gp, 0, t - 1)
            self.stack_tile(gp, 0, T - 1)
            self.max_row(gp, 0, 0)

        def pair(self, b, i, par, search, prep, first):
            gp = PAIRS * b + i
            self.exp(gp, 0, 0)
            self.max_row(gp, par, 1)
            for t in range(T):
                if t < T - 1:
                    self.exp(gp, 0, t + 1)
                else:
                    self.exp(gp, 1, 0)
                    self.out_move(gp, 0)
                if t == 0 and not first:
                    self.out_rows(gp - 1, i - 1, 0)
                if prep:
                    self.prep_tile(gp + 1, 1 - par, t)
                    if t > 0:
                        self.stack_tile(gp + 1, 1 - par, t - 1)
                if t == 0 and not first:
                    self.out_rows(gp - 1, i - 1, 1)
            for t in range(T):
                if t < T - 1:
                    self.exp(gp, 1, t + 1)
                if prep and t == 1:
                    self.stack_tile(gp + 1, 1 - par, T - 1)
                if prep and t == T // 2:
                    self.max_row(gp + 1, 1 - par, 0)
            self.out_move(gp, 1)

        def finish(self):
            pass

    class Vector:
        def __init__(self, e):
            self.e = e

        def setup(self):
            e = self.e
            e.memset(mz[:].bitcast(F32), 0.0).then_inc(c_cst, 1)
            e.memset(cnt[:], 0.0).then_inc(z_cnt, CST)
            for t in range(T):
                self.keys_first(0, t)
                if t > 0:
                    self.keys_last(0, t - 1)
            self.keys_last(0, T - 1)

        def conditioning(self):
            e = self.e
            e.wait_ge(c_cnd, 1)
            e.wait_ge(c_parT, 1)
            bias = paramsT[:, NC:NC + 16].unsqueeze(2).broadcast_to([P, 16, B])
            e.tensor_tensor(gain[:], pax[:, 1, 0:16 * B].rearrange("p (k b) -> p k b", b=B), bias,
                            ALU.add).then_inc(c_cndT, 1)
            e.wait_ge(c_cndT, 1)
            g = paramsT[:, NC + 16:NC + 24].unsqueeze(2).broadcast_to([P, KT, B])
            e.scalar_tensor_tensor(gain[:, 0:KT, :], gain[:, 0:KT, :], 1.0, g, ALU.add, ALU.mult).then_inc(c_cndT, 1)

        def keys_first(self, b, t):
            e, k, c = self.e, T * b + t, slice(t, t + 1)
            e.wait_ge(d_key[t], 16 * (b + 1))
            e.tensor_reduce(kmx[:, c], keys[:, t, :], axis=AX, op=ALU.max).then_inc(k_max, 1)
            e.wait_ge(k_max, 2 * k + 1)
            e.tensor_scalar(knm[:, c], kmx[:, c], -1.0, None, ALU.mult).then_inc(k_max, 1)

        def keys_last(self, b, t):
            e, k, c = self.e, T * b + t, slice(t, t + 1)
            e.wait_ge(k_exp, k + 1)
            e.reciprocal(krz[:, c], kz[:, c]).then_inc(k_key, 1)
            e.wait_ge(d_s, 16)
            e.wait_ge(k_key, 3 * k + 1)
            e.scalar_tensor_tensor(kw[:, c], krz[:, c], 1.0 / N ** 0.5, s_sb[:, bass.ds(b, 1), t], ALU.mult, ALU.mult).then_inc(k_key, 1)
            e.wait_ge(d_tb, 16 * (b + 1))
            e.wait_ge(k_key, 3 * k + 2)
            e.scalar_tensor_tensor(keys[:, t, :], tb[:], kw[:, c], keys[:, t, :], ALU.mult, ALU.mult).then_inc(k_key, 1)

        def search_init(self, b):
            e = self.e
            e.wait_ge(k_diag, T * (b + 1))
            e.memset(prefix[:], 0)
            e.memset(bit[:], SIGN)
            e.memset(cand[:], SIGN)
            e.memset(thr[:], 0).then_inc(z_init, 1)
            e.wait_ge(z_init, b + 1)

        def search_count(self, z, c):
            e = self.e
            kv = keys[:].rearrange("p t n -> p (t n)")[:, c * CHUNK:(c + 1) * CHUNK]
            e.wait_ge(z_cnt, CST + 4 * z + c - 1)
            e.tensor_scalar(trash[:, c % 2, :], kv, thr_f, None, ALU.is_ge, ALU.add,
                            accum_out=cnt[:, c:c + 1]).then_inc(z_cnt, 1)

        def search_update(self, z):
            e, n = self.e, 6 * z
            e.wait_ge(z_sum, z + 1)
            e.tensor_reduce(tot[:], tot4[:], axis=AX, op=ALU.add).then_inc(z_up, 1)
            e.wait_ge(z_up, n + 1)
            e.tensor_scalar(acc[:], tot[:], TOPK - 0.5, None, ALU.is_ge).then_inc(z_up, 1)
            e.wait_ge(z_up, n + 2)
            e.tensor_scalar(bit[:], bit[:], 1, None, ALU.logical_shift_right)
            e.copy_predicated(prefix[:], acc[:], cand[:]).then_inc(z_up, 1)
            e.wait_ge(z_up, n + 3)
            e.tensor_tensor(cand[:], prefix[:], bit[:], ALU.bitwise_or).then_inc(z_up, 1)
            e.wait_ge(z_up, n + 4)
            e.tensor_scalar(flip[:], cand[:], 31, -1, ALU.arith_shift_right, ALU.bitwise_xor).then_inc(z_up, 1)
            e.wait_ge(z_up, n + 5)
            e.scalar_tensor_tensor(thr[:], flip[:], SIGN, cand[:], ALU.bitwise_or, ALU.bitwise_xor).then_inc(z_up, 1)
            e.wait_ge(z_up, n + 6)

        def search_alone(self, b):
            self.search_init(b)
            with self.e.Fori(0, STEPS) as st:
                z = STEPS * b + st
                for c in range(4):
                    self.search_count(z, c)
                self.search_update(z)

        def boundary(self, ob, fb):
            e = self.e
            if ob is not None:
                e.wait_ge(d_wo, 16 * (ob + 1))
                for k in range(KT):
                    i = e.tensor_tensor(wo[:, k, k * P:(k + 1) * P], wo[:, k, k * P:(k + 1) * P], ident, ALU.add)
                i.then_inc(o_wi, 1)
            if fb is not None:
                n = F_STEPS * fb
                kv = keys[:].rearrange("p t n -> p (t n)")
                if ob is None:
                    self.conditioning()
                for j, op in enumerate((ALU.is_gt, ALU.is_equal)):
                    for c in range(4):
                        if 4 * j + c >= 2:
                            e.wait_ge(f_dve, n + 4 * j + c - 1)
                        e.tensor_scalar(trash[:, c % 2, :], kv[:, c * CHUNK:(c + 1) * CHUNK], thr_f, None, op, ALU.add,
                                        accum_out=cnt[:, 4 * j + c:4 * j + c + 1]).then_inc(f_dve, 1)
                e.wait_ge(f_sum, fb + 1)
                e.tensor_reduce(ngt[:], gt4[:], axis=AX, op=ALU.add).then_inc(f_dve, 1)
                e.wait_ge(f_tri, fb + 1)
                e.tensor_reduce(pre[:], ppv[:, 0, 0:4], axis=AX, op=ALU.add).then_inc(f_dve, 1)
                e.wait_ge(f_dve, n + 10)
                e.tensor_tensor(r0[:], ngt[:], pre[:], ALU.add).then_inc(f_dve, 1)
                e.wait_ge(f_dve, n + 11)
                e.tensor_scalar(rank[:], r0[:], -1.0, float(TOPK), ALU.mult, ALU.add).then_inc(f_dve, 1)
                e.wait_ge(f_dve, n + 12)
            for t in range(T):
                if fb is not None:
                    self.finalise_tile(fb, t)
                if ob is not None:
                    self.project_tile(ob, t)
            if fb is not None:
                for j in range(2):
                    e.wait_ge(d_x1[j], 16 * (T // 2) * (fb + 1))

        def finalise_tile(self, b, t):
            e, n = self.e, F_STEPS * b + 12 + 4 * t
            if t > 0:
                e.tensor_copy(carry[:], scn[:, N - 1:N]).then_inc(f_dve, 1)
            else:
                e.memset(carry[:], 0.0).then_inc(f_dve, 1)
            e.tensor_scalar(eqm[:], keys[:, t, :], thr_f, None, ALU.is_equal).then_inc(f_dve, 1)
            e.wait_ge(f_dve, n + 2)
            e.tensor_tensor_scan(scn[:], eqm[:], eqm[:], carry[:], ALU.add, ALU.max).then_inc(f_dve, 1)
            e.wait_ge(f_dve, n + 3)
            e.scalar_tensor_tensor(eqm[:], scn[:], rank[:], eqm[:], ALU.is_le, ALU.mult).then_inc(f_dve, 1)
            e.wait_ge(d_xin[t % 2], 16 * (T // 2 * b + t // 2 + 1))
            e.scalar_tensor_tensor(xin[:, t % 2, :], keys[:, t, :], thr_f, xin[:, t % 2, :],
                                   ALU.is_gt, ALU.add).then_inc(f_x1m, 1)
            e.wait_ge(f_dve, n + 4)
            e.wait_ge(f_x1m, T * b + t + 1)
            e.tensor_tensor(xin[:, t % 2, :], xin[:, t % 2, :], eqm[:], ALU.add).then_inc(f_x1, 1)
            e.wait_ge(f_rs, 2 * (T * b + t) + 2)
            e.tensor_scalar(xr[:, t % 4, :], xin[:, t % 2, :], rsx[:, t:t + 1], None, ALU.mult).then_inc(f_xr, 1)

        def project_tile(self, b, t):
            e = self.e
            for c in range(2):
                q = 2 * T * b + 2 * t + c
                e.wait_ge(o_mm, q + 1)
                e.wait_ge(d_res[c], 16 * (T * b + t + 1))
                if t > 0:
                    e.wait_ge(d_y[c], 16 * (T * b + t))
                cols = slice(c * HALF, (c + 1) * HALF)
                e.tensor_tensor(yout[:, cols], pst[:, (2 * t + c) % 4, :], xres[:, cols], ALU.add).then_inc(o_add, 1)

        def prep_sums(self, gp, t):
            e, u = self.e, T * gp + t
            e.wait_ge(a_sq, u + 1)
            e.tensor_reduce(ss[:], sq[:], axis=AX, op=ALU.add).then_inc(a_ss, 1)

        def prep_split(self, gp, t):
            e, u = self.e, T * gp + t
            e.wait_ge(a_rs, 2 * u + 2)
            for h in range(4):
                i = e.scalar_tensor_tensor(qkn[:, h, :], qkn[:, h, :], rs[:, h:h + 1],
                                           gqk[:, h // 2, :], ALU.mult, ALU.mult)
            i.then_inc(a_nm, 1)
            wait(e, a_tr, u)
            e.wait_ge(a_nm, 3 * u + 1)
            st = stage[:]
            e.tensor_copy(st[:, 0:2, 0:DH], qkn[:, 0:2, :])
            e.tensor_copy(st[:, 2:4, DH:P], qkn[:, 2:4, :]).then_inc(a_nm, 1)
            e.wait_ge(a_nm, 3 * u + 2)
            e.tensor_tensor(st[:, 0:2, DH:P], qkn[:, 0:2, :], st[:, 0:2, 0:DH].bitcast(F32), ALU.subtract)
            e.tensor_tensor(st[:, 2:4, 0:DH], qkn[:, 2:4, :], st[:, 2:4, DH:P].bitcast(F32),
                            ALU.subtract).then_inc(a_nm, 1)

        def row_max(self, gp, j, alone=False):
            e, v = self.e, 4 * T * gp + 2 * j
            for c in range(2):
                e.wait_ge(m_s, v + c + 1)
                e.tensor_reduce(mx2[:, j // T, j % T, c:c + 1], max_banks(alone, j)[:, c, :], axis=AX,
                                op=ALU.max).then_inc(m_mx, 1)
            if j % T == T - 1:
                e.wait_ge(m_mx, v + 2)
                e.tensor_reduce(mz[:, j // T, DH:DH + T], mx2[:, j // T, :, :], axis=AX, op=ALU.max).then_inc(m_cb, 1)

        def normalise(self, gp, hh):
            e, g = self.e, 2 * gp + hh
            e.wait_ge(t_tk, g + 1)
            ov = ppv[:, :, 0:4 * (DH + 1)].rearrange("p a (q d) -> p a q d", q=4)
            rv = rl[:].rearrange("p (a q) -> p a q", a=2)
            e.reciprocal(rv, ov[:, :, :, DH]).then_inc(t_rl, 1)
            e.wait_ge(t_rl, g + 1)
            for a in range(2):
                i = e.tensor_tensor(otok[:, 4 * a:4 * a + 4, hh * DH:(hh + 1) * DH], ov[:, a, :, 0:DH],
                                    rv[:, a, :].unsqueeze(2).broadcast_to([P, 4, DH]), ALU.mult)
            i.then_inc(t_on, 1)

        def prep_alone(self, b, kb):
            gp = PAIRS * b
            for t in range(T):
                if kb is not None:
                    self.keys_first(kb, t)
                self.prep_sums(gp, t)
                if kb is not None and t > 0:
                    self.keys_last(kb, t - 1)
                self.prep_split(gp, t)
            if kb is not None:
                self.keys_last(kb, T - 1)
            for j in range(2 * T):
                self.row_max(gp, j, True)

        def pair(self, b, i, par, search, prep, first):
            gp = PAIRS * b + i
            if search and first:
                self.search_init(b + 1)
            for t in range(T):
                z = STEPS * (b + 1) + 4 * i + t // 2
                last = prep and t == T - 1
                if search:
                    self.search_count(z, 2 * (t % 2))
                    if t % 2 == 1 and not last:
                        self.search_count(z, 3)
                if prep:
                    self.prep_sums(gp + 1, t)
                if search and t % 2 == 0:
                    self.search_count(z, 1)
                elif search and not last:
                    self.search_update(z)
                if t == (T - 1 if prep or not search else T // 2 - 1):
                    self.normalise(gp, 0)
                if prep:
                    self.prep_split(gp + 1, t)
                if search and last:
                    self.search_count(z, 3)
                    self.search_update(z)
            if prep:
                for j in range(2 * T):
                    self.row_max(gp + 1, j)
            self.normalise(gp, 1)

        def finish(self):
            pass

    class Tensor:
        def __init__(self, e):
            self.e = e

        def setup(self):
            e = self.e
            e.wait_ge(d_par, 48)
            e.wait_ge(c_pool, 4)
            e.transpose(pax[:, 0, 0:NC + 24], params, ident[0:NC + 24, 0:NC + 24]).then_inc(c_par, 1)
            e.wait_ge(c_parT, 1)
            e.wait_ge(d_wemb, 16)
            ct = paramsT[:, 0:NC].rearrange("p (b k) -> p k b", k=KT)
            for j in range(2 * KT):
                for k in range(KT):
                    i = e.matmul(pax[:, 1, j * B:(j + 1) * B], wemb_v[:, k, j * P:(j + 1) * P], ct[:, k, 0:B],
                                 start=(k == 0), stop=(k == KT - 1))
            i.then_inc(c_cnd, 1)
            e.wait_ge(c_cst, 1)
            e.matmul(ppv[:, 1, 0:P], ident, ident, start=True, stop=True).then_inc(t_pv, CST)

        def search_alone(self, b):
            pass

        def boundary(self, ob, fb):
            e = self.e
            if ob is not None:
                self.out_tokens(PAIRS * ob + PAIRS - 1, 1)
                for h in range(2):
                    self.out_rows(PAIRS * ob + PAIRS - 1, h)
                e.wait_ge(t_oe, 2 * PAIRS * (ob + 1))
                e.wait_ge(o_wi, ob + 1)
                e.wait_ge(t_on, 2 * PAIRS * (ob + 1))
            for t in range(T):
                if ob is not None:
                    self.project_tile(ob, t, 0)
                if fb is not None and t == 0:
                    self.before(fb)
                if ob is not None:
                    self.project_tile(ob, t, 1)
                if fb is not None and t % 4 == 3:
                    self.features(fb, t // 4)

        def before(self, b):
            e = self.e
            e.wait_ge(f_dve, F_STEPS * b + 8)
            e.matmul(ppv[:, 0, 0:4], tri[:], cnt[:, 4:8], start=True, stop=True).then_inc(f_tri, 1)

        def features(self, b, g):
            e = self.e
            e.wait_ge(f_xr, T * b + 4 * g + 4)
            for k in range(KT):
                n = 2 * KT * b + KT * g + k
                if k > 1 or g:
                    e.wait_ge(f_ev, n - 1)
                for j in range(4):
                    i = e.transpose(ppv[:, k % 2, j * P:(j + 1) * P], xr[:, j, k * P:(k + 1) * P], ident)
                i.then_inc(f_xt, 1)

        def project_tile(self, b, t, c):
            e, q = self.e, 2 * T * b + 2 * t + c
            if 2 * t + c >= 4:
                e.wait_ge(o_add, q - 3)
            for k in range(KT):
                i = e.matmul(pst[:, (2 * t + c) % 4, :], oT[:, k, t * P:(t + 1) * P],
                             wo[:, k, c * HALF:(c + 1) * HALF], start=(k == 0), stop=(k == KT - 1))
            i.then_inc(o_mm, 1)

        def prep_tile(self, gp, t, alone=False):
            e, u = self.e, T * gp + t
            if t == 0:
                e.wait_ge(d_w, 48 * (gp + 1))
            elif t > 1 or not alone:
                e.wait_ge(a_v, u - 1 if alone else u)
            for k in range(KT):
                i = e.matmul(qkv_bank(alone, t)[:, 0:6 * DH], xnT[:, k, t * P:(t + 1) * P],
                             wq[:, k, :, :].rearrange("p s c -> p (s c)"), start=(k == 0), stop=(k == KT - 1))
            i.then_inc(a_qkv, 1)

        def transpose_tile(self, gp, t):
            e, u = self.e, T * gp + t
            e.wait_ge(a_nm, 3 * u + 3)
            if t > 0:
                e.wait_ge(a_ev, u)
            for h in range(4):
                i = e.transpose(paxr[:, 1, h * P:(h + 1) * P], stage[:, h, :], identr[:])
            i.then_inc(a_tr, 1)

        def score_max(self, gp, par, j, alone=False):
            e, v = self.e, 4 * T * gp + 2 * j
            if j == 0:
                e.wait_ge(a_ev, T * (gp + 1))
                e.wait_ge(a_row, 2 * (gp + 1))
            elif j == T + alone:
                e.wait_ge(m_ev, 2 * gp + 1)
            hh, qt = j // T, j % T
            for c in range(2):
                if j == T and alone or j % T and not alone:
                    e.wait_ge(m_mx, v + c - 1)
                elif alone and j > 1 and j != T + 1:
                    e.wait_ge(m_mx, v + c - 3)
                e.matmul(max_banks(alone, j)[:, c, :], sA[par][0:DH + 1, hh, qt * P:(qt + 1) * P],
                         sA[par][0:DH + 1, 2 + hh, c * HALF:(c + 1) * HALF], start=True, stop=True).then_inc(m_s, 1)

        def max_row(self, gp, hh):
            e = self.e
            e.wait_ge(m_cb, 2 * gp + hh + 1)
            for q in range(T):
                i = e.matmul(pax[0:DH + 1, q // 4, (q % 4) * P:(q % 4 + 1) * P], mz[:, hh, q:q + DH + 1],
                             identr[:], start=True, stop=True)
            i.then_inc(m_row, 1)

        def scores(self, gp, par, hh, kt):
            e, w = self.e, T * (2 * gp + hh) + kt
            if kt == 0:
                e.wait_ge(m_ev, 2 * gp + hh + 1)
            e.wait_ge(t_ex, CST + w - 1)
            for m, (op, k) in enumerate(((sA[par], DH + 1), (sB[par], P))):
                for c in range(2):
                    i = e.matmul(pst[:, 2 * (kt % 2) + c, :], op[0:k, 2 + hh, kt * P:(kt + 1) * P],
                                 op[0:k, hh, c * HALF:(c + 1) * HALF], start=(m == 0), stop=(m == 1),
                                 skip_group_check=True)
            i.then_inc(t_st, 1)

        def values(self, gp, par, hh, kt, between=None):
            e, w = self.e, T * (2 * gp + hh) + kt
            if kt == 0:
                wait(e, t_on, 2 * gp + hh)
            e.wait_ge(t_ex, CST + w + 1)
            for c in range(2):
                i = e.matmul(ppv[0:DH + 1, c, :], v2[:, par, kt, hh, :], pt[:, kt % 2, c * HALF:(c + 1) * HALF],
                             start=(kt == 0), stop=(kt == T - 1))
                if c == 0 and between is not None:
                    between()
            i.then_inc(t_pv, 1)

        def out_tokens(self, gp, hh):
            e, g = self.e, 2 * gp + hh
            e.wait_ge(t_mv, g + 1)
            for q in range(T):
                c = (q % 4) * (DH + 1)
                i = e.transpose(ppv[:, q // 4, c:c + DH + 1], heads_t[:, q * P:(q + 1) * P],
                                ident[0:DH + 1, 0:DH + 1])
            i.then_inc(t_tk, 1)

        def out_rows(self, gp, h):
            e = self.e
            if h == 0:
                e.wait_ge(t_on, 2 * gp + 2)
            else:
                e.wait_ge(t_oe, 2 * gp + 1)
            for t in range(4):
                i = e.transpose(pax[:, 1, t * P:(t + 1) * P], otok[:, 4 * h + t, :], ident)
            i.then_inc(t_ot, 1)

        def prep_alone(self, b, kb):
            e, gp = self.e, PAIRS * b
            wait(e, t_oe, 2 * gp)
            e.wait_ge(f_ev, 2 * KT * (b + 1))
            if isinstance(gp, int) and gp == 0:
                e.wait_ge(c_cndT, 2)
                e.wait_ge(d_gqk, 32)
            for t in range(T):
                self.prep_tile(gp, t, True)
                if t > 0:
                    self.transpose_tile(gp, t - 1)
            self.transpose_tile(gp, T - 1)
            for j in range(2 * T):
                self.score_max(gp, 0, j, True)
                if j == T:
                    self.max_row(gp, 0)

        def pair(self, b, i, par, search, prep, first):
            e, gp = self.e, PAIRS * b + i
            self.scores(gp, par, 0, 0)
            if not first:
                self.out_tokens(gp - 1, 1)
            self.max_row(gp, 1)
            for t in range(T):
                if t < T - 1:
                    self.scores(gp, par, 0, t + 1)
                else:
                    self.scores(gp, par, 1, 0)
                self.values(gp, par, 0, t)
                if t == 0:
                    e.wait_ge(m_ev, 2 * gp + 2)
                    if not first:
                        self.out_rows(gp - 1, 0)
                if prep:
                    self.prep_tile(gp + 1, t)
                if t == 0 and not first:
                    self.out_rows(gp - 1, 1)
                if prep and t > 0:
                    if t == 1 and not first:
                        e.wait_ge(t_oe, 2 * gp)
                    self.transpose_tile(gp + 1, t - 1)
            gaps = ["row" if n == 9 else (n if n < 8 else n - 2 if n > 9 else None)
                    for n in range(3 * T - 6)] if prep else [None] * (3 * T - 6)

            def fill():
                what = gaps.pop(0)
                if what == "row":
                    self.max_row(gp + 1, 0)
                elif what is not None:
                    self.score_max(gp + 1, 1 - par, what)

            self.out_tokens(gp, 0)
            self.scores(gp, par, 1, 1)
            self.scores(gp, par, 1, 2)
            self.values(gp, par, 1, 0)
            if prep:
                self.transpose_tile(gp + 1, T - 1)
            self.values(gp, par, 1, 1)
            fill()
            for t in range(2, T):
                if t < T - 1:
                    self.scores(gp, par, 1, t + 1)
                    fill()
                self.values(gp, par, 1, t, fill)
                fill()

        def finish(self):
            pass

    F_STEPS = 12 + 4 * T
    f_x1m = sem("f_x1m")

    def batch(s, b, search, fb, kb):
        s.pair(b, 0, 0, search, True, True)
        with s.e.Fori(0, (PAIRS - 2) // 2) as ii:
            s.pair(b, 2 * ii + 1, 1, search, True, False)
            s.pair(b, 2 * ii + 2, 0, search, True, False)
        s.pair(b, PAIRS - 1, 1, search, False, False)
        s.boundary(b, fb)
        if fb is not None:
            s.prep_alone(fb, kb)

    def program(s):
        s.setup()
        s.search_alone(0)
        s.boundary(None, 0)
        s.prep_alone(0, 1 if B > 1 else None)
        if B > 2:
            with s.e.Fori(0, B - 2) as b:
                batch(s, b, True, b + 1, b + 2)
        if B > 1:
            batch(s, B - 2, True, B - 1, None)
        batch(s, B - 1, False, None, None)
        s.finish()

    with nc.Block() as block:
        @block.sync
        def _(e):
            program(Sync(e))

        @block.gpsimd
        def _(e):
            program(Pool(e))

        @block.scalar
        def _(e):
            program(Scalar(e))

        @block.vector
        def _(e):
            program(Vector(e))

        @block.tensor
        def _(e):
            program(Tensor(e))


NAMES = ["x", "fside_BxSx1_0", "cond_2048", "L1_cond_W_emb", "L1_cond_b_emb", "L1_cond_g_norm",
         "L1_cond_W_qkv", "L1_cond_g_q", "L1_cond_g_k", "L1_cond_W_out"]


def kernel(**inputs):
    import numpy as np
    import concourse.bacc as bacc
    from concourse.bass_utils import run_bass_kernel_spmd

    nc = bacc.Bacc("TRN2", target_bir_lowering=False, num_devices=1)
    arrays, args = {}, []
    for name in NAMES:
        a = np.ascontiguousarray(inputs[name])
        arrays[f"in_{name}"] = a
        args.append(nc.dram_tensor(f"in_{name}", a.shape, mybir.dt.from_np(a.dtype), kind="ExternalInput").ap())
    args.append(nc.dram_tensor("out_x", arrays["in_x"].shape, F32, kind="ExternalOutput").ap())
    with ExitStack() as ctx:
        cond_block(nc, *args, ctx)
    r = run_bass_kernel_spmd(nc, [arrays], core_ids=[0])
    return r.results[0]["out_x"]
```

```python
from contextlib import ExitStack

import concourse.bass as bass
from concourse import mybir

F32 = mybir.dt.float32
F32R = mybir.dt.float32r
BF16 = mybir.dt.bfloat16
I32 = mybir.dt.int32
U8 = mybir.dt.uint8
ALU = mybir.AluOpType
ACT = mybir.ActivationFunctionType
AX = mybir.AxisListType.X
ADD_ALL = bass.bass_isa.ReduceOp.add
P = 128
LOWEST = -3.4028234663852886e38
SIGN = -2147483648


def wait(e, sem, value):
    if not isinstance(value, int) or value > 0:
        e.wait_ge(sem, value)


def wait_apart(e, sem, value, passed):
    e.wait_ge(sem, value)
    e.sem_inc(passed, 1)


def cond_block(nc, x, s_in, cond, w_emb, b_emb, g_norm, w_qkv, g_q, g_k, w_out, out, ctx):
    B, N, D = x.shape
    T = N // P
    KT = D // P
    DH = g_q.shape[0]
    HEADS = D // DH
    PAIRS = HEADS // 2
    TOPK = 10240
    STEPS = 32
    UNROLL = 8
    WARM = 12
    EPS = 1e-6
    HALF = N // 2
    CHUNK = T * N // 4
    NC = B * KT
    assert T == 8 and KT == 8 and PAIRS == 8 and HALF == 512 and DH == 64

    def sem(name):
        return ctx.enter_context(nc.semaphore(name))

    def sb(name, shape, dt=F32):
        return ctx.enter_context(nc.sbuf_tensor(name, shape, dt))

    keys = sb("keys", [P, T, N])
    feat = sb("feat", [P, 2 * KT, N])
    xnT, oT = feat[:, 0:KT, :], feat[:, KT:2 * KT, :]
    wemb_v = feat[:].rearrange("p k n -> p (k n)").rearrange("p (k n) -> p k n", k=KT)
    wq = sb("wq", [P, KT, 3, P])
    v2 = sb("v2", [P, 2, T, 2, DH + 1])
    pt = sb("pt", [P, 2, N])
    stage = sb("stage", [P, 4, P], F32R)
    sq = sb("sq", [P, 4, DH])
    qkn = sb("qkn", [P, 4, DH])
    otok = sb("otok", [P, T, P])
    trash = sb("trash", [P, 2, CHUNK], U8)
    gqk = sb("gqk", [P, 2, DH])
    identr = sb("identr", [P, P], F32R)
    ident = identr[:].bitcast(F32)
    heads_t = sb("heads_t", [DH + 1, N])
    tri = sb("tri", [P, P])
    mz = sb("mz", [P, 2, DH + T], F32R)
    mx2 = sb("mx2", [P, 2, T, 2])
    paramsT = sb("paramsT", [P, NC + 24])
    gain = sb("gain", [P, 2 * KT, B])
    s_sb = sb("s_sb", [P, B, T])
    small = {n: sb(n, [P, w]) for n, w in dict(
        ss=4, rs=4, half4=4, rl=T, kmx=T, knm=T, kz=T, krz=T, kw=T, cnt=8, tot4=4, tot=1, eq4=4, neq=1, reach=1,
        pre=1, r0=1, rank=1, carry=1, ssx=T, rsx=T).items()}
    ss, rs, half4, rl = (small[n] for n in ("ss", "rs", "half4", "rl"))
    kmx, knm, kz, krz, kw = (small[n] for n in ("kmx", "knm", "kz", "krz", "kw"))
    cnt, tot4, tot, eq4, neq, reach, pre, r0, rank, carry, ssx, rsx = (
        small[n] for n in ("cnt", "tot4", "tot", "eq4", "neq", "reach", "pre", "r0", "rank", "carry", "ssx", "rsx"))
    state = sb("state", [P, 3], I32)
    prefix, cand, thr = state[:, 0:1], state[:, 1:2], state[:, 2:3]
    bit, flip, acc = (sb(n, [P, 1], I32) for n in ("bit", "flip", "acc"))
    ahead = sb("ahead", [P, 2, 3], I32)
    flip2 = sb("flip2", [P, 2], I32)
    thr_f = thr.bitcast(F32)
    inner = ExitStack()
    sB0 = inner.enter_context(nc.sbuf_tensor("sB0", [P, 4, N], F32R))
    sA0 = inner.enter_context(nc.sbuf_tensor("sA0", [P, 4, N], F32R))
    sB1 = inner.enter_context(nc.sbuf_tensor("sB1", [P, 4, N], F32R))
    sA1 = inner.enter_context(nc.sbuf_tensor("sA1", [P, 4, N], F32R))
    inner.close()
    sA, sB = [sA0, sA1], [sB0, sB1]
    wo = sb("wo", [P, KT, N])
    xin = sb("xin", [P, 2, N])
    xr = sb("xr", [P, 4, N])
    eqm = sb("eqm", [P, N])
    scn = sb("scn", [P, N])
    params = scn[0:NC + 24, 0:P]
    tb = eqm
    mask = xr[:].rearrange("p a n -> p (a n)").bitcast(BF16)
    ones = stage[:].rearrange("p a n -> p (a n)").bitcast(BF16)[:, 0:HALF]
    mask_cuts = [0, 3072, 5632, 7168, T * N]
    cond_rows = pt[0:B, :, :]
    xres, yout = pt[:, 0, :], pt[:, 1, :]

    pst = ctx.enter_context(nc.psum_tensor("pst", [P, 4, HALF], F32))
    ppv = ctx.enter_context(nc.psum_tensor("ppv", [P, 2, HALF], F32))
    pax = ctx.enter_context(nc.psum_tensor("pax", [P, 2, HALF], F32))
    paxr = pax[:].bitcast(F32R)

    d_par, d_wemb, d_gqk, d_s, d_tb, d_w, d_wo = (
        sem(n) for n in ("d_par", "d_wemb", "d_gqk", "d_s", "d_tb", "d_w", "d_wo"))
    d_key = [sem(f"d_key{t}") for t in range(T)]
    d_xin = [sem(f"d_xin{t}") for t in range(2)]
    d_x1 = [sem(f"d_x1{t}") for t in range(2)]
    d_res = [sem(f"d_res{t}") for t in range(2)]
    d_y = [sem(f"d_y{t}") for t in range(2)]
    c_pool, c_cst, c_par, c_parT, c_cnd, c_rows, c_cndT = (
        sem(n) for n in ("c_pool", "c_cst", "c_par", "c_parT", "c_cnd", "c_rows", "c_cndT"))
    k_max, k_key, k_exp, k_diag = sem("k_max"), sem("k_key"), sem("k_exp"), sem("k_diag")
    passed = sem("passed")
    y_mask, y_sum, y_up = sem("y_mask"), sem("y_sum"), sem("y_up")
    z_init, z_cnt, z_sum, z_up = sem("z_init"), sem("z_cnt"), sem("z_sum"), sem("z_up")
    f_dve, f_sum, f_tri, f_x1, f_sq, f_rs, f_xr, f_xt, f_ev = (
        sem(n) for n in ("f_dve", "f_sum", "f_tri", "f_x1", "f_sq", "f_rs", "f_xr", "f_xt", "f_ev"))
    a_qkv, a_sq, a_v, a_ss, a_rs, a_nm, a_tr, a_ev, a_row = (
        sem(n) for n in ("a_qkv", "a_sq", "a_v", "a_ss", "a_rs", "a_nm", "a_tr", "a_ev", "a_row"))
    m_s, m_mx, m_cb, m_row, m_ev = (sem(n) for n in ("m_s", "m_mx", "m_cb", "m_row", "m_ev"))
    t_st, t_ex, t_pv, t_mv, t_tk, t_rl, t_on, t_ot, t_oe = (
        sem(n) for n in ("t_st", "t_ex", "t_pv", "t_mv", "t_tk", "t_rl", "t_on", "t_ot", "t_oe"))
    o_wi, o_mm, o_add = sem("o_wi"), sem("o_mm"), sem("o_add")

    x_v = x.rearrange("b (p t) n -> b p t n", t=T)
    out_v = out.rearrange("b (p t) n -> b p t n", t=T)
    wqkv_v = w_qkv.rearrange("(k p) (s i c) -> p k s i c", p=P, s=3, i=PAIRS)

    def qkv_bank(alone, t):
        return ppv[:, 0, :] if alone and t % 2 else pax[:, 0, :]

    def max_banks(alone, j):
        return ppv if alone and (j + j // T) % 2 else pax

    CST = 2

    class Sync:
        def __init__(self, e):
            self.e = e

        def setup(self):
            e = self.e
            e.dma_start(s_sb[:], s_in.rearrange("b (p t) a -> p b (t a)", t=T)).then_inc(d_s, 16)
            self.load_keys(0)
            e.dma_start(params[0:NC, :], cond.rearrange("b (k p) -> (b k) p", p=P)).then_inc(d_par, 16)
            e.dma_start(params[NC:NC + 16, :], b_emb.rearrange("(k p) -> k p", p=P)).then_inc(d_par, 16)
            e.dma_start(params[NC + 16:NC + 24, :], g_norm.rearrange("(k p) -> k p", p=P)).then_inc(d_par, 16)
            e.dma_start(gqk[:, 0, :], g_q.partition_broadcast(P)).then_inc(d_gqk, 16)
            e.dma_start(gqk[:, 1, :], g_k.partition_broadcast(P)).then_inc(d_gqk, 16)
            e.dma_start(wemb_v, w_emb.rearrange("(k p) n -> p k n", p=P)).then_inc(d_wemb, 16)
            self.load_w(0)

        def load_keys(self, b):
            e = self.e
            for t in range(T):
                e.dma_start(keys[:, t, :], x_v[b, :, t, :]).then_inc(d_key[t], 16)
                if t == 0:
                    e.dma_start(tb[:], cond[b, :].partition_broadcast(P)).then_inc(d_tb, 16)

        def load_w(self, i):
            for s in range(3):
                self.e.dma_start(wq[:, :, s, :], wqkv_v[:, :, s, i, :]).then_inc(d_w, 16)

        def search_alone(self, b):
            pass

        def x_tile(self, b, t):
            self.e.dma_start(xin[:, t % 2, :], x_v[b, :, t, :]).then_inc(d_xin[t % 2], 16)

        def finalise_tile(self, b, t):
            e = self.e
            e.wait_ge(f_x1, T * b + t + 1)
            e.dma_start(out_v[b, :, t, :], xin[:, t % 2, :]).then_inc(d_x1[t % 2], 16)
            if t + 2 < T:
                e.wait_ge(d_x1[t % 2], 16 * (T // 2 * b + t // 2 + 1))
                e.wait_ge(f_xr, T * b + t + 1)
                self.x_tile(b, t + 2)

        def boundary(self, ob, fb):
            e = self.e
            if ob is not None:
                wait_apart(e, t_pv, CST + T * 2 * PAIRS * (ob + 1), passed)
                for j in range(2):
                    e.wait_ge(d_x1[j], 16 * (T // 2) * (ob + 1))
                for c in range(2):
                    self.residual(ob, 0, c)
            if fb is not None:
                self.x_tile(fb, 0)
                self.x_tile(fb, 1)
            for t in range(T):
                if fb is not None:
                    self.finalise_tile(fb, t)
                if ob is not None:
                    for c in range(2):
                        e.wait_ge(o_add, 2 * T * ob + 2 * t + c + 1)
                        e.dma_start(out_v[ob, :, t, c * HALF:(c + 1) * HALF],
                                    yout[:, c * HALF:(c + 1) * HALF]).then_inc(d_y[c], 16)
                        if t + 1 < T:
                            self.residual(ob, t + 1, c)

        def residual(self, b, t, c):
            self.e.dma_start(xres[:, c * HALF:(c + 1) * HALF],
                             out_v[b, :, t, c * HALF:(c + 1) * HALF]).then_inc(d_res[c], 16)

        def prep_alone(self, b, kb):
            e = self.e
            if kb is not None:
                e.wait_ge(f_xr, T * (b + 1))
                self.load_keys(kb)
            e.wait_ge(a_qkv, T * (PAIRS * b + 1))
            self.load_w(1)

        def pair(self, b, i, par, search, prep, first):
            e, gp = self.e, PAIRS * b + i
            if prep:
                wait_apart(e, a_qkv, T * (gp + 2), passed)
                self.load_w((i + 2) % PAIRS)
            else:
                e.wait_ge(t_pv, CST + 2 * T * gp)
                e.dma_start(wo[:], w_out.rearrange("(k p) n -> p k n", p=P)).then_inc(d_wo, 16)

        def finish(self):
            for c in range(2):
                self.e.wait_ge(d_y[c], 16 * T * B)
                self.e.wait_ge(d_x1[c], 16 * T // 2 * B)

    class Pool:
        def __init__(self, e):
            self.e = e

        def setup(self):
            e = self.e
            e.memset(scn[:, P:2 * P], 0.0).then_inc(c_pool, 1)
            e.memset(tri[:], 1.0).then_inc(c_pool, 1)
            e.memset(half4[:], -0.5).then_inc(c_pool, 1)
            e.wait_ge(c_pool, 3)
            e.affine_select(out=identr[:], in_=scn[:, P:2 * P], compare_op=ALU.not_equal, fill=1.0, base=0,
                            pattern=[[-1, P]], channel_multiplier=1).then_inc(c_pool, 1)
            e.affine_select(out=tri[:], in_=tri[:], compare_op=ALU.is_gt, fill=0.0, base=0,
                            pattern=[[1, P]], channel_multiplier=-1).then_inc(c_pool, 1)
            e.memset(v2[:, :, :, :, DH:DH + 1], 1.0).then_inc(c_pool, 1)
            e.memset(ones, 1.0).then_inc(c_pool, 1)
            for t in range(T):
                self.keys_tile(0, t)

        def keys_tile(self, b, t):
            e, k = self.e, T * b + t
            wait_apart(e, k_key, 3 * k + 3, passed)
            e.affine_select(out=keys[:, t, :], in_=keys[:, t, :], compare_op=ALU.not_equal, fill=LOWEST,
                            base=t, pattern=[[-1, N]], channel_multiplier=T).then_inc(k_diag, 1)
            wait_apart(e, k_diag, k + 1, passed)

        def search_alone(self, b):
            pass

        def search_sum(self, z):
            e = self.e
            wait_apart(e, z_cnt, CST + 4 * z + 4, passed)
            e.partition_all_reduce(tot4[:], cnt[:, 0:4], P, ADD_ALL).then_inc(z_sum, 1)

        def boundary(self, ob, fb):
            e = self.e
            if fb is None:
                return
            wait_apart(e, f_dve, F_STEPS * fb + 4, passed)
            e.partition_all_reduce(eq4[:], cnt[:, 4:8], P, ADD_ALL).then_inc(f_sum, 1)
            for t in range(T):
                n = T * fb + t
                wait_apart(e, f_sq, n + 1, passed)
                e.tensor_scalar(rsx[:, t:t + 1], ssx[:, t:t + 1], 1.0 / D, EPS, ALU.mult, ALU.add).then_inc(f_rs, 1)
                e.wait_ge(f_rs, 2 * n + 1)
                e.tensor_tensor(rsx[:, t:t + 1], rsx[:, t:t + 1], half4[:, 0:1], ALU.pow).then_inc(f_rs, 1)

        def prep_tile(self, gp, t):
            e, u = self.e, T * gp + t
            wait_apart(e, a_ss, u + 1, passed)
            e.tensor_scalar(rs[:], ss[:], 1.0 / DH, EPS, ALU.mult, ALU.add).then_inc(a_rs, 1)
            e.wait_ge(a_rs, 2 * u + 1)
            e.tensor_tensor(rs[:], rs[:], half4[:], ALU.pow).then_inc(a_rs, 1)

        def prep_rows(self, gp, par):
            e = self.e
            wait_apart(e, a_qkv, T * gp + 1, passed)
            e.memset(sA[par][DH:DH + 1, 0:2, :].bitcast(F32), 0.0).then_inc(a_row, 1)
            e.memset(sA[par][DH:DH + 1, 2:4, :].bitcast(F32), -1.0).then_inc(a_row, 1)
            wait_apart(e, a_row, 2 * (gp + 1), passed)

        def prep_alone(self, b, kb):
            gp = PAIRS * b
            for t in range(T):
                self.prep_tile(gp, t)
                if t == 0:
                    wait_apart(self.e, a_rs, 2 * T * gp + 2, passed)
                    self.prep_rows(gp, 0)
                if kb is not None and t > 0:
                    self.keys_tile(kb, t - 1)
            if kb is not None:
                self.keys_tile(kb, T - 1)

        def pair(self, b, i, par, search, prep, first):
            e, gp = self.e, PAIRS * b + i
            if prep:
                self.prep_rows(gp + 1, 1 - par)
            else:
                wait_apart(e, d_wo, 16 * (b + 1), passed)
                for k in range(KT):
                    cols = slice(k * P, (k + 1) * P)
                    w = e.tensor_tensor(wo[:, k, cols], wo[:, k, cols], ident, ALU.add)
                w.then_inc(o_wi, 1)
            for t in range(T):
                last = prep and t == T - 1
                if search and t % 2 == 1 and not last:
                    self.search_sum(STEPS * b + 4 * i + t // 2)
                if prep:
                    self.prep_tile(gp + 1, t)
                if search and last:
                    z = STEPS * b + 4 * i + t // 2
                    self.search_sum(z)
                    wait_apart(e, z_sum, z + 1, passed)

        def finish(self):
            pass

    class Scalar:
        def __init__(self, e):
            self.e = e

        def setup(self):
            e = self.e
            for t in range(T):
                self.keys_tile(0, t)
            e.wait_ge(c_pool, 3)
            e.activation(carry[:], half4[:, 0:1], ACT.Copy).then_inc(t_ex, CST)
            e.wait_ge(c_par, 1)
            e.activation(paramsT[:], pax[:, 0, 0:NC + 24], ACT.Copy).then_inc(c_parT, 1)

        def keys_tile(self, b, t):
            e, k = self.e, T * b + t
            e.wait_ge(k_max, 2 * k + 2)
            e.activation(keys[:, t, :], keys[:, t, :], ACT.Exp, bias=knm[:, t:t + 1],
                         accum_out=kz[:, t:t + 1]).then_inc(k_exp, 1)

        def search_alone(self, b):
            pass

        def boundary(self, ob, fb):
            e = self.e
            if ob is not None:
                for h in range(2):
                    self.out_rows(PAIRS * ob + PAIRS - 1, PAIRS - 1, h)
            if fb is not None:
                for g in range(2):
                    for t in range(4 * g, 4 * g + 4):
                        e.wait_ge(f_x1, T * fb + t + 1)
                        if g:
                            e.wait_ge(f_xt, 2 * KT * fb + KT)
                        e.activation(xr[:, t % 4, :], xin[:, t % 2, :], ACT.Square,
                                     accum_out=ssx[:, t:t + 1]).then_inc(f_sq, 1)
                        e.wait_ge(f_rs, 2 * (T * fb + t) + 2)
                        e.activation(xr[:, t % 4, :], xin[:, t % 2, :], ACT.Copy,
                                     scale=rsx[:, t:t + 1]).then_inc(f_xr, 1)
                    if ob is None and g == 0:
                        e.wait_ge(c_cnd, 1)
                        e.activation(cond_rows.rearrange("b a n -> b (a n)"),
                                     pst[0:B, :, :].rearrange("b a n -> b (a n)"), ACT.Copy).then_inc(c_rows, 1)
                        e.wait_ge(c_cndT, 2)
                    for k in range(KT):
                        wait_apart(e, f_xt, 2 * KT * fb + KT * g + k + 1, passed)
                        e.activation(xnT[:, k, g * HALF:(g + 1) * HALF], ppv[:, k % 2, :], ACT.Identity,
                                     scale=gain[:, k, bass.ds(fb, 1)],
                                     bias=gain[:, KT + k, bass.ds(fb, 1)]).then_inc(f_ev, 1)
            if ob is not None:
                for c in range(2):
                    e.wait_ge(d_y[c], 16 * T * (ob + 1))

        def prep_tile(self, gp, par, t, alone=False):
            e, u = self.e, T * gp + t
            bank = qkv_bank(alone, t)
            e.wait_ge(a_qkv, u + 1)
            wait(e, a_nm, 3 * u)
            e.activation(qkn[:].rearrange("p h d -> p (h d)"), bank[:, 0:4 * DH], ACT.Copy)
            e.activation(sq[:].rearrange("p h d -> p (h d)"), bank[:, 0:4 * DH], ACT.Square).then_inc(a_sq, 1)
            e.activation(v2[:, par, t, :, 0:DH], bank[:, 4 * DH:6 * DH].rearrange("p (h d) -> p h d", h=2),
                         ACT.Copy).then_inc(a_v, 1)

        def stack_tile(self, gp, par, t):
            e, u = self.e, T * gp + t
            e.wait_ge(a_tr, u + 1)
            src = pax[:, 1, :].rearrange("p (h c) -> p h c", h=4)
            cols = slice(t * P, (t + 1) * P)
            e.activation(sB[par][:, :, cols], src, ACT.Copy)
            e.activation(sA[par][0:DH, 2:4, cols], src[DH:P, 2:4, :], ACT.Copy)
            e.activation(sA[par][0:DH, 0:2, cols], src[0:DH, 0:2, :], ACT.Copy).then_inc(a_ev, 1)

        def max_row(self, gp, par, hh):
            e = self.e
            e.wait_ge(m_row, 2 * gp + hh + 1)
            e.activation(sA[par][DH:DH + 1, hh, :], pax[DH:DH + 1, :, :].rearrange("p a b -> p (a b)"),
                         ACT.Copy).then_inc(m_ev, 1)

        def exp(self, gp, hh, kt):
            e, w = self.e, T * (2 * gp + hh) + kt
            e.wait_ge(t_st, w + 1)
            e.wait_ge(t_pv, CST + w - 1)
            e.activation(pt[:, kt % 2, :], pst[:, 2 * (kt % 2):2 * (kt % 2) + 2, :].rearrange("p a b -> p (a b)"),
                         ACT.Exp, scale=DH ** -0.5).then_inc(t_ex, 1)

        def out_move(self, gp, hh):
            e, g = self.e, 2 * gp + hh
            e.wait_ge(t_pv, CST + T * (g + 1))
            e.activation(heads_t[:], ppv[0:DH + 1, :, :].rearrange("p a b -> p (a b)"), ACT.Copy).then_inc(t_mv, 1)

        def out_rows(self, gp, i, h):
            e = self.e
            wait_apart(e, t_ot, 2 * gp + h + 1, passed)
            e.activation(oT[:, i, h * HALF:(h + 1) * HALF], pax[:, 1, :], ACT.Copy).then_inc(t_oe, 1)

        def prep_alone(self, b, kb):
            gp = PAIRS * b
            for t in range(T):
                self.prep_tile(gp, 0, t, True)
                if kb is not None:
                    self.keys_tile(kb, t)
                if t > 0:
                    self.stack_tile(gp, 0, t - 1)
            self.stack_tile(gp, 0, T - 1)
            self.max_row(gp, 0, 0)

        def pair(self, b, i, par, search, prep, first):
            gp = PAIRS * b + i
            self.exp(gp, 0, 0)
            self.max_row(gp, par, 1)
            for t in range(T):
                if t < T - 1:
                    self.exp(gp, 0, t + 1)
                else:
                    self.exp(gp, 1, 0)
                    self.out_move(gp, 0)
                if t == 0 and not first:
                    self.out_rows(gp - 1, i - 1, 0)
                if prep:
                    self.prep_tile(gp + 1, 1 - par, t)
                    if t > 0:
                        self.stack_tile(gp + 1, 1 - par, t - 1)
                if t == 0 and not first:
                    self.out_rows(gp - 1, i - 1, 1)
            for t in range(T):
                if t < T - 1:
                    self.exp(gp, 1, t + 1)
                if prep and t == 1:
                    self.stack_tile(gp + 1, 1 - par, T - 1)
                if prep and t == T // 2:
                    self.max_row(gp + 1, 1 - par, 0)
            self.out_move(gp, 1)

        def finish(self):
            pass

    class Vector:
        def __init__(self, e):
            self.e = e

        def setup(self):
            e = self.e
            e.memset(mz[:].bitcast(F32), 0.0).then_inc(c_cst, 1)
            e.memset(cnt[:], 0.0).then_inc(z_cnt, CST)
            e.memset(kz[:], 0.0).then_inc(t_on, CST)
            for t in range(T):
                self.keys_first(0, t)
                if t > 0:
                    self.keys_last(0, t - 1)
            self.keys_last(0, T - 1)

        def conditioning(self):
            e = self.e
            e.wait_ge(c_cnd, 2)
            e.wait_ge(c_parT, 1)
            bias = paramsT[:, NC:NC + 16].unsqueeze(2).broadcast_to([P, 16, B])
            e.tensor_tensor(gain[:], pax[:, 1, 0:16 * B].rearrange("p (k b) -> p k b", b=B), bias,
                            ALU.add).then_inc(c_cndT, 1)
            e.wait_ge(c_cndT, 1)
            g = paramsT[:, NC + 16:NC + 24].unsqueeze(2).broadcast_to([P, KT, B])
            e.scalar_tensor_tensor(gain[:, 0:KT, :], gain[:, 0:KT, :], 1.0, g, ALU.add, ALU.mult).then_inc(c_cndT, 1)

        def keys_first(self, b, t):
            e, k, c = self.e, T * b + t, slice(t, t + 1)
            e.wait_ge(d_key[t], 16 * (b + 1))
            e.tensor_reduce(kmx[:, c], keys[:, t, :], axis=AX, op=ALU.max).then_inc(k_max, 1)
            e.wait_ge(k_max, 2 * k + 1)
            e.tensor_scalar(knm[:, c], kmx[:, c], -1.0, None, ALU.mult).then_inc(k_max, 1)

        def keys_last(self, b, t):
            e, k, c = self.e, T * b + t, slice(t, t + 1)
            e.wait_ge(k_exp, k + 1)
            e.reciprocal(krz[:, c], kz[:, c]).then_inc(k_key, 1)
            e.wait_ge(d_s, 16)
            e.wait_ge(k_key, 3 * k + 1)
            e.scalar_tensor_tensor(kw[:, c], krz[:, c], 1.0 / N ** 0.5, s_sb[:, bass.ds(b, 1), t],
                                   ALU.mult, ALU.mult).then_inc(k_key, 1)
            e.wait_ge(d_tb, 16 * (b + 1))
            e.wait_ge(k_key, 3 * k + 2)
            e.scalar_tensor_tensor(keys[:, t, :], tb[:], kw[:, c], keys[:, t, :], ALU.mult, ALU.mult).then_inc(k_key, 1)

        def search_init(self, b):
            e = self.e
            e.wait_ge(k_diag, T * (b + 1))
            e.memset(prefix, 0)
            e.memset(reach[:], float(N * N))
            e.memset(bit[:], SIGN)
            e.memset(cand, SIGN)
            e.memset(thr, 0).then_inc(z_init, 1)
            e.wait_ge(z_init, b + 1)

        def search_count(self, z, c):
            e = self.e
            kv = keys[:].rearrange("p t n -> p (t n)")[:, c * CHUNK:(c + 1) * CHUNK]
            e.wait_ge(z_cnt, CST + 4 * z + c - 1)
            e.tensor_scalar(trash[:, c % 2, :], kv, thr_f, None, ALU.is_ge, ALU.add,
                            accum_out=cnt[:, c:c + 1]).then_inc(z_cnt, 1)

        def search_update(self, z):
            e, n = self.e, 6 * z
            e.wait_ge(z_sum, z + 1)
            e.tensor_reduce(tot[:], tot4[:], axis=AX, op=ALU.add).then_inc(z_up, 1)
            e.wait_ge(z_up, n + 1)
            e.tensor_scalar(acc[:], tot[:], TOPK - 0.5, None, ALU.is_ge).then_inc(z_up, 1)
            e.wait_ge(z_up, n + 2)
            e.tensor_scalar(bit[:], bit[:], 1, None, ALU.logical_shift_right)
            e.copy_predicated(reach[:], acc[:], tot[:])
            e.copy_predicated(prefix, acc[:], cand).then_inc(z_up, 1)
            e.wait_ge(z_up, n + 3)
            e.tensor_tensor(cand, prefix, bit[:], ALU.bitwise_or).then_inc(z_up, 1)
            e.wait_ge(z_up, n + 4)
            e.tensor_scalar(flip[:], cand, 31, -1, ALU.arith_shift_right, ALU.bitwise_xor).then_inc(z_up, 1)
            e.wait_ge(z_up, n + 5)
            e.scalar_tensor_tensor(thr, flip[:], SIGN, cand, ALU.bitwise_or, ALU.bitwise_xor).then_inc(z_up, 1)
            wait_apart(e, z_up, n + 6, passed)

        def search_alone(self, b):
            e = self.e
            self.search_init(b)
            kv = keys[:].rearrange("p t n -> p (t n)")
            parts = len(mask_cuts) - 1
            with e.Fori(0, STEPS // UNROLL) as q:
                for r in range(UNROLL):
                    z = UNROLL * q + r
                    n = 7 * z
                    for lo, hi in zip(mask_cuts, mask_cuts[1:]):
                        e.tensor_scalar(mask[:, lo:hi], kv[:, lo:hi], thr_f, None, ALU.is_ge).then_inc(y_mask, 1)
                    e.tensor_scalar(bit[:], bit[:], 1, None, ALU.logical_shift_right).then_inc(y_up, 1)
                    e.tensor_copy(ahead[:, :, 0], state[:, 0:2])
                    e.wait_ge(y_up, n + 1)
                    e.tensor_tensor(ahead[:, :, 1], state[:, 0:2], bit[:].broadcast_to([P, 2]),
                                    ALU.bitwise_or).then_inc(y_up, 1)
                    e.wait_ge(y_up, n + 2)
                    e.tensor_scalar(flip2[:], ahead[:, :, 1], 31, -1, ALU.arith_shift_right,
                                    ALU.bitwise_xor).then_inc(y_up, 1)
                    e.wait_ge(y_up, n + 3)
                    e.scalar_tensor_tensor(ahead[:, :, 2], flip2[:], SIGN, ahead[:, :, 1], ALU.bitwise_or,
                                           ALU.bitwise_xor).then_inc(y_up, 1)
                    e.wait_ge(y_mask, parts * (z + 1))
                    e.wait_ge(y_up, n + 4)
                    e.tensor_copy(state[:], ahead[:, 0, :])
                    e.wait_ge(y_sum, z + 1)
                    e.tensor_reduce(tot[:], pst[:, 0, :], axis=AX, op=ALU.add).then_inc(y_up, 1)
                    e.wait_ge(y_up, n + 5)
                    e.tensor_scalar(acc[:], tot[:], TOPK - 0.5, None, ALU.is_ge).then_inc(y_up, 1)
                    wait_apart(e, y_up, n + 6, passed)
                    e.copy_predicated(reach[:], acc[:], tot[:])
                    e.copy_predicated(state[:], acc[:].broadcast_to([P, 3]), ahead[:, 1, :]).then_inc(y_up, 1)
                    wait_apart(e, y_up, n + 7, passed)

        def boundary(self, ob, fb):
            e = self.e
            if fb is not None:
                n = F_STEPS * fb
                kv = keys[:].rearrange("p t n -> p (t n)")
                for c in range(4):
                    if c > 1:
                        e.wait_ge(f_dve, n + c - 1)
                    e.tensor_scalar(trash[:, c % 2, :], kv[:, c * CHUNK:(c + 1) * CHUNK], thr_f, None, ALU.is_equal,
                                    ALU.add, accum_out=cnt[:, 4 + c:5 + c]).then_inc(f_dve, 1)
                e.wait_ge(f_sum, fb + 1)
                e.tensor_reduce(neq[:], eq4[:], axis=AX, op=ALU.add).then_inc(f_dve, 1)
                e.wait_ge(f_tri, fb + 1)
                e.tensor_reduce(pre[:], ppv[:, 0, 0:4], axis=AX, op=ALU.add).then_inc(f_dve, 1)
                e.wait_ge(f_dve, n + 6)
                e.scalar_tensor_tensor(r0[:], pre[:], neq[:], reach[:], ALU.subtract, ALU.add).then_inc(f_dve, 1)
                e.wait_ge(f_dve, n + 7)
                e.tensor_scalar(rank[:], r0[:], -1.0, float(TOPK), ALU.mult, ALU.add).then_inc(f_dve, 1)
                e.wait_ge(f_dve, n + 8)
            for t in range(T):
                if fb is not None:
                    self.finalise_tile(fb, t)
                    if ob is None and t == T // 2:
                        self.conditioning()
                if ob is not None:
                    self.project_tile(ob, t)
            if fb is not None:
                for j in range(2):
                    e.wait_ge(d_x1[j], 16 * (T // 2) * (fb + 1))

        def finalise_tile(self, b, t):
            e, n = self.e, F_STEPS * b + 8 + 4 * t
            if t > 0:
                e.tensor_copy(carry[:], scn[:, N - 1:N]).then_inc(f_dve, 1)
            else:
                e.memset(carry[:], 0.0).then_inc(f_dve, 1)
            wait(e, f_x1, T * b + t)
            e.tensor_scalar(eqm[:], keys[:, t, :], thr_f, None, ALU.is_equal).then_inc(f_dve, 1)
            e.wait_ge(f_dve, n + 2)
            e.tensor_tensor_scan(scn[:], eqm[:], eqm[:], carry[:], ALU.add, ALU.max).then_inc(f_dve, 1)
            e.wait_ge(f_dve, n + 3)
            e.scalar_tensor_tensor(eqm[:], scn[:], rank[:], eqm[:], ALU.is_le, ALU.mult).then_inc(f_dve, 1)
            e.wait_ge(d_xin[t % 2], 16 * (T // 2 * b + t // 2 + 1))
            e.scalar_tensor_tensor(xin[:, t % 2, :], keys[:, t, :], thr_f, xin[:, t % 2, :],
                                   ALU.is_gt, ALU.add).then_inc(f_x1m, 1)
            e.wait_ge(f_dve, n + 4)
            e.wait_ge(f_x1m, T * b + t + 1)
            e.tensor_tensor(xin[:, t % 2, :], xin[:, t % 2, :], eqm[:], ALU.add).then_inc(f_x1, 1)

        def project_tile(self, b, t):
            e = self.e
            for c in range(2):
                q = 2 * T * b + 2 * t + c
                e.wait_ge(o_mm, q + 1)
                e.wait_ge(d_res[c], 16 * (T * b + t + 1))
                if t > 0:
                    e.wait_ge(d_y[c], 16 * (T * b + t))
                cols = slice(c * HALF, (c + 1) * HALF)
                e.tensor_tensor(yout[:, cols], pst[:, (2 * t + c) % 4, :], xres[:, cols], ALU.add).then_inc(o_add, 1)

        def prep_sums(self, gp, t):
            e, u = self.e, T * gp + t
            e.wait_ge(a_sq, u + 1)
            e.tensor_reduce(ss[:], sq[:], axis=AX, op=ALU.add).then_inc(a_ss, 1)

        def prep_split(self, gp, t):
            e, u = self.e, T * gp + t
            e.wait_ge(a_rs, 2 * u + 2)
            for h in range(4):
                i = e.scalar_tensor_tensor(qkn[:, h, :], qkn[:, h, :], rs[:, h:h + 1],
                                           gqk[:, h // 2, :], ALU.mult, ALU.mult)
            i.then_inc(a_nm, 1)
            wait(e, a_tr, u)
            e.wait_ge(a_nm, 3 * u + 1)
            st = stage[:]
            e.tensor_copy(st[:, 0:2, 0:DH], qkn[:, 0:2, :])
            e.tensor_copy(st[:, 2:4, DH:P], qkn[:, 2:4, :]).then_inc(a_nm, 1)
            e.wait_ge(a_nm, 3 * u + 2)
            e.tensor_tensor(st[:, 0:2, DH:P], qkn[:, 0:2, :], st[:, 0:2, 0:DH].bitcast(F32), ALU.subtract)
            e.tensor_tensor(st[:, 2:4, 0:DH], qkn[:, 2:4, :], st[:, 2:4, DH:P].bitcast(F32),
                            ALU.subtract).then_inc(a_nm, 1)

        def row_max(self, gp, j, alone=False):
            e, v = self.e, 4 * T * gp + 2 * j
            for c in range(2):
                e.wait_ge(m_s, v + c + 1)
                e.tensor_reduce(mx2[:, j // T, j % T, c:c + 1], max_banks(alone, j)[:, c, :], axis=AX,
                                op=ALU.max).then_inc(m_mx, 1)
            if j % T == T - 1:
                e.wait_ge(m_mx, v + 2)
                e.tensor_reduce(mz[:, j // T, DH:DH + T], mx2[:, j // T, :, :], axis=AX, op=ALU.max).then_inc(m_cb, 1)

        def normalise(self, gp, hh):
            e, g = self.e, 2 * gp + hh
            e.wait_ge(t_tk, g + 1)
            ov = ppv[:, :, 0:4 * (DH + 1)].rearrange("p a (q d) -> p a q d", q=4)
            rv = rl[:].rearrange("p (a q) -> p a q", a=2)
            e.reciprocal(rv, ov[:, :, :, DH]).then_inc(t_rl, 1)
            e.wait_ge(t_rl, g + 1)
            for a in range(2):
                i = e.tensor_tensor(otok[:, 4 * a:4 * a + 4, hh * DH:(hh + 1) * DH], ov[:, a, :, 0:DH],
                                    rv[:, a, :].unsqueeze(2).broadcast_to([P, 4, DH]), ALU.mult)
            i.then_inc(t_on, 1)

        def prep_alone(self, b, kb):
            gp = PAIRS * b
            for t in range(T):
                if kb is not None:
                    self.keys_first(kb, t)
                self.prep_sums(gp, t)
                if kb is not None and t > 0:
                    self.keys_last(kb, t - 1)
                self.prep_split(gp, t)
            if kb is not None:
                self.keys_last(kb, T - 1)
            for j in range(2 * T):
                self.row_max(gp, j, True)

        def pair(self, b, i, par, search, prep, first):
            gp = PAIRS * b + i
            if search and first:
                self.search_init(b + 1)
            for t in range(T):
                z = STEPS * b + 4 * i + t // 2
                last = prep and t == T - 1
                if search:
                    self.search_count(z, 2 * (t % 2))
                if not prep and t in (T // 2 - 1, T - 1):
                    self.normalise(gp, t // (T // 2))
                if search:
                    if t % 2 == 1 and not last:
                        self.search_count(z, 3)
                if prep:
                    self.prep_sums(gp + 1, t)
                if search and t % 2 == 0:
                    self.search_count(z, 1)
                elif search and not last:
                    self.search_update(z)
                if prep and t == T - 1:
                    self.normalise(gp, 0)
                if prep:
                    self.prep_split(gp + 1, t)
            if prep:
                for j in range(2 * T):
                    self.row_max(gp + 1, j)
                self.normalise(gp, 1)
            if search and prep:
                self.search_count(z, 3)
                self.search_update(z)

        def finish(self):
            pass

    class Tensor:
        def __init__(self, e):
            self.e = e

        def setup(self):
            e = self.e
            e.wait_ge(d_par, 48)
            e.wait_ge(c_pool, 4)
            e.transpose(pax[:, 0, 0:NC + 24], params, ident[0:NC + 24, 0:NC + 24]).then_inc(c_par, 1)
            e.wait_ge(c_parT, 1)
            e.wait_ge(c_cst, 1)
            e.matmul(ppv[:, 1, 0:P], ident, ident, start=True, stop=True).then_inc(t_pv, CST)

        def search_alone(self, b):
            e = self.e
            e.wait_ge(c_pool, 7)
            cuts = mask_cuts[1:]
            with e.Fori(0, STEPS // UNROLL) as q:
                for r in range(UNROLL):
                    z = UNROLL * q + r
                    for j in range(T * N // HALF):
                        c = sum(j * HALF >= cut for cut in cuts)
                        e.wait_ge(y_mask, len(cuts) * z + c + 1)
                        i = e.matmul(pst[:, 0, :], ones[:, 0:P], mask[:, j * HALF:(j + 1) * HALF],
                                     start=(j == 0), stop=(j == T * N // HALF - 1))
                    i.then_inc(y_sum, 1)
                    for _ in range(WARM):
                        e.matmul(pst[:, 1, :], ones[:, 0:P], ones, start=True, stop=True)

        def conditioning(self):
            e = self.e
            e.wait_ge(d_wemb, 16)
            ct = paramsT[:, 0:NC].rearrange("p (b k) -> p k b", k=KT)
            for c in range(4):
                for k in range(KT):
                    i = e.matmul(pst[0:B, c, :], ct[:, k, 0:B], wemb_v[:, k, c * HALF:(c + 1) * HALF],
                                 start=(k == 0), stop=(k == KT - 1))
            i.then_inc(c_cnd, 1)
            e.wait_ge(c_rows, 1)
            rows = cond_rows.rearrange("b a n -> b (a n)")
            for j in range(2 * KT):
                i = e.transpose(pax[:, 1, j * B:(j + 1) * B], rows[:, j * P:(j + 1) * P], ident[0:B, 0:B])
            i.then_inc(c_cnd, 1)

        def boundary(self, ob, fb):
            e = self.e
            if ob is not None:
                self.out_tokens(PAIRS * ob + PAIRS - 1, 1)
                for h in range(2):
                    self.out_rows(PAIRS * ob + PAIRS - 1, h)
                e.wait_ge(t_oe, 2 * PAIRS * (ob + 1))
                e.wait_ge(o_wi, ob + 1)
                e.wait_ge(t_on, CST + 2 * PAIRS * (ob + 1))
            for t in range(T):
                if ob is not None:
                    self.project_tile(ob, t, 0)
                if fb is not None and t == 0:
                    self.before(fb)
                    if ob is None:
                        self.conditioning()
                if ob is not None:
                    self.project_tile(ob, t, 1)
                if fb is not None and t % 4 == 3:
                    self.features(fb, t // 4)

        def before(self, b):
            e = self.e
            e.wait_ge(f_dve, F_STEPS * b + 4)
            e.matmul(ppv[:, 0, 0:4], tri[:], cnt[:, 4:8], start=True, stop=True).then_inc(f_tri, 1)

        def features(self, b, g):
            e = self.e
            e.wait_ge(f_xr, T * b + 4 * g + 4)
            for k in range(KT):
                n = 2 * KT * b + KT * g + k
                if k > 1 or g:
                    e.wait_ge(f_ev, n - 1)
                for j in range(4):
                    i = e.transpose(ppv[:, k % 2, j * P:(j + 1) * P], xr[:, j, k * P:(k + 1) * P], ident)
                i.then_inc(f_xt, 1)

        def project_tile(self, b, t, c):
            e, q = self.e, 2 * T * b + 2 * t + c
            if 2 * t + c >= 4:
                e.wait_ge(o_add, q - 3)
            for k in range(KT):
                i = e.matmul(pst[:, (2 * t + c) % 4, :], oT[:, k, t * P:(t + 1) * P],
                             wo[:, k, c * HALF:(c + 1) * HALF], start=(k == 0), stop=(k == KT - 1))
            i.then_inc(o_mm, 1)

        def prep_tile(self, gp, t, alone=False):
            e, u = self.e, T * gp + t
            if t == 0:
                e.wait_ge(d_w, 48 * (gp + 1))
            elif t > 1 or not alone:
                e.wait_ge(a_v, u - 1 if alone else u)
            for k in range(KT):
                i = e.matmul(qkv_bank(alone, t)[:, 0:6 * DH], xnT[:, k, t * P:(t + 1) * P],
                             wq[:, k, :, :].rearrange("p s c -> p (s c)"), start=(k == 0), stop=(k == KT - 1))
            i.then_inc(a_qkv, 1)

        def transpose_tile(self, gp, t):
            e, u = self.e, T * gp + t
            e.wait_ge(a_nm, 3 * u + 3)
            if t > 0:
                e.wait_ge(a_ev, u)
            for h in range(4):
                i = e.transpose(paxr[:, 1, h * P:(h + 1) * P], stage[:, h, :], identr[:])
            i.then_inc(a_tr, 1)

        def score_max(self, gp, par, j, alone=False):
            e, v = self.e, 4 * T * gp + 2 * j
            if j == 0:
                e.wait_ge(a_ev, T * (gp + 1))
                e.wait_ge(a_row, 2 * (gp + 1))
            elif j == T + alone:
                e.wait_ge(m_ev, 2 * gp + 1)
            hh, qt = j // T, j % T
            for c in range(2):
                if j == T and alone or j % T and not alone:
                    e.wait_ge(m_mx, v + c - 1)
                elif alone and j > 1 and j != T + 1:
                    e.wait_ge(m_mx, v + c - 3)
                e.matmul(max_banks(alone, j)[:, c, :], sA[par][0:DH + 1, hh, qt * P:(qt + 1) * P],
                         sA[par][0:DH + 1, 2 + hh, c * HALF:(c + 1) * HALF], start=True, stop=True).then_inc(m_s, 1)

        def max_row(self, gp, hh):
            e = self.e
            e.wait_ge(m_cb, 2 * gp + hh + 1)
            for q in range(T):
                i = e.matmul(pax[0:DH + 1, q // 4, (q % 4) * P:(q % 4 + 1) * P], mz[:, hh, q:q + DH + 1],
                             identr[:], start=True, stop=True)
            i.then_inc(m_row, 1)

        def scores(self, gp, par, hh, kt):
            e, w = self.e, T * (2 * gp + hh) + kt
            if kt == 0:
                e.wait_ge(m_ev, 2 * gp + hh + 1)
            e.wait_ge(t_ex, CST + w - 1)
            for m, (op, k) in enumerate(((sA[par], DH + 1), (sB[par], P))):
                for c in range(2):
                    i = e.matmul(pst[:, 2 * (kt % 2) + c, :], op[0:k, 2 + hh, kt * P:(kt + 1) * P],
                                 op[0:k, hh, c * HALF:(c + 1) * HALF], start=(m == 0), stop=(m == 1),
                                 skip_group_check=True)
            i.then_inc(t_st, 1)

        def values(self, gp, par, hh, kt, between=None):
            e, w = self.e, T * (2 * gp + hh) + kt
            if kt == 0:
                e.wait_ge(t_on, CST + 2 * gp + hh)
            e.wait_ge(t_ex, CST + w + 1)
            for c in range(2):
                i = e.matmul(ppv[0:DH + 1, c, :], v2[:, par, kt, hh, :], pt[:, kt % 2, c * HALF:(c + 1) * HALF],
                             start=(kt == 0), stop=(kt == T - 1))
                if c == 0 and between is not None:
                    between()
            i.then_inc(t_pv, 1)

        def out_tokens(self, gp, hh):
            e, g = self.e, 2 * gp + hh
            e.wait_ge(t_mv, g + 1)
            for q in range(T):
                c = (q % 4) * (DH + 1)
                i = e.transpose(ppv[:, q // 4, c:c + DH + 1], heads_t[:, q * P:(q + 1) * P],
                                ident[0:DH + 1, 0:DH + 1])
            i.then_inc(t_tk, 1)

        def out_rows(self, gp, h):
            e = self.e
            if h == 0:
                e.wait_ge(t_on, CST + 2 * gp + 2)
            else:
                e.wait_ge(t_oe, 2 * gp + 1)
            for t in range(4):
                i = e.transpose(pax[:, 1, t * P:(t + 1) * P], otok[:, 4 * h + t, :], ident)
            i.then_inc(t_ot, 1)

        def prep_alone(self, b, kb):
            e, gp = self.e, PAIRS * b
            wait(e, t_oe, 2 * gp)
            e.wait_ge(f_ev, 2 * KT * (b + 1))
            if isinstance(gp, int) and gp == 0:
                e.wait_ge(c_cndT, 2)
                e.wait_ge(d_gqk, 32)
            for t in range(T):
                self.prep_tile(gp, t, True)
                if t > 0:
                    self.transpose_tile(gp, t - 1)
            self.transpose_tile(gp, T - 1)
            for j in range(2 * T):
                self.score_max(gp, 0, j, True)
                if j == T:
                    self.max_row(gp, 0)

        def pair(self, b, i, par, search, prep, first):
            e, gp = self.e, PAIRS * b + i
            self.scores(gp, par, 0, 0)
            if not first:
                self.out_tokens(gp - 1, 1)
            self.max_row(gp, 1)
            for t in range(T):
                if t < T - 1:
                    self.scores(gp, par, 0, t + 1)
                else:
                    self.scores(gp, par, 1, 0)
                self.values(gp, par, 0, t)
                if t == 0:
                    e.wait_ge(m_ev, 2 * gp + 2)
                    if not first:
                        self.out_rows(gp - 1, 0)
                if prep:
                    self.prep_tile(gp + 1, t)
                if t == 0 and not first:
                    self.out_rows(gp - 1, 1)
                if prep and t > 0:
                    if t == 1 and not first:
                        e.wait_ge(t_oe, 2 * gp)
                    self.transpose_tile(gp + 1, t - 1)
            gaps = ["row" if n == 9 else (n if n < 8 else n - 2 if n > 9 else None)
                    for n in range(3 * T - 6)] if prep else [None] * (3 * T - 6)

            def fill():
                what = gaps.pop(0)
                if what == "row":
                    self.max_row(gp + 1, 0)
                elif what is not None:
                    self.score_max(gp + 1, 1 - par, what)

            self.out_tokens(gp, 0)
            self.scores(gp, par, 1, 1)
            self.scores(gp, par, 1, 2)
            self.values(gp, par, 1, 0)
            if prep:
                self.transpose_tile(gp + 1, T - 1)
            self.values(gp, par, 1, 1)
            fill()
            for t in range(2, T):
                if t < T - 1:
                    self.scores(gp, par, 1, t + 1)
                    fill()
                self.values(gp, par, 1, t, fill)
                fill()

        def finish(self):
            pass

    F_STEPS = 8 + 4 * T
    f_x1m = sem("f_x1m")

    def batch(s, b, search, fb, kb):
        s.pair(b, 0, 0, search, True, True)
        with s.e.Fori(0, (PAIRS - 2) // 2) as ii:
            s.pair(b, 2 * ii + 1, 1, search, True, False)
            s.pair(b, 2 * ii + 2, 0, search, True, False)
        s.pair(b, PAIRS - 1, 1, search, False, False)
        s.boundary(b, fb)
        if fb is not None:
            s.prep_alone(fb, kb)

    def program(s):
        s.setup()
        s.search_alone(0)
        s.boundary(None, 0)
        s.prep_alone(0, 1 if B > 1 else None)
        if B > 2:
            with s.e.Fori(0, B - 2) as b:
                batch(s, b, True, b + 1, b + 2)
        if B > 1:
            batch(s, B - 2, True, B - 1, None)
        batch(s, B - 1, False, None, None)
        s.finish()

    with nc.Block() as block:
        @block.sync
        def _(e):
            program(Sync(e))

        @block.gpsimd
        def _(e):
            program(Pool(e))

        @block.scalar
        def _(e):
            program(Scalar(e))

        @block.vector
        def _(e):
            program(Vector(e))

        @block.tensor
        def _(e):
            program(Tensor(e))


NAMES = ["x", "fside_BxSx1_0", "cond_2048", "L1_cond_W_emb", "L1_cond_b_emb", "L1_cond_g_norm",
         "L1_cond_W_qkv", "L1_cond_g_q", "L1_cond_g_k", "L1_cond_W_out"]


def kernel(**inputs):
    import numpy as np
    import concourse.bacc as bacc
    from concourse.bass_utils import run_bass_kernel_spmd

    nc = bacc.Bacc("TRN2", target_bir_lowering=False, num_devices=1)
    arrays, args = {}, []
    for name in NAMES:
        a = np.ascontiguousarray(inputs[name])
        arrays[f"in_{name}"] = a
        args.append(nc.dram_tensor(f"in_{name}", a.shape, mybir.dt.from_np(a.dtype), kind="ExternalInput").ap())
    args.append(nc.dram_tensor("out_x", arrays["in_x"].shape, F32, kind="ExternalOutput").ap())
    with ExitStack() as ctx:
        cond_block(nc, *args, ctx)
    r = run_bass_kernel_spmd(nc, [arrays], core_ids=[0])
    return r.results[0]["out_x"]
```
